# Optimizing a Trainium2 kernel written in Bass

```python
import numpy as np
import jax
import jax.numpy as jnp

def _softmax(x, axis=-1):
    return jax.nn.softmax(x, axis=axis)

def _gelu(x):
    return jax.nn.gelu(x, approximate=True)

def _silu(x):
    return jax.nn.silu(x)

def _sigmoid(x):
    return jax.nn.sigmoid(x)

def _layernorm(x, axis=-1, eps=1e-05):
    m = jnp.mean(x, axis=axis, keepdims=True)
    v = jnp.var(x, axis=axis, keepdims=True)
    return (x - m) / jnp.sqrt(v + eps)

def _scatter_add(tgt, idx, src, axis=0):
    return tgt.at[idx].add(src)

def _segment_sum(src, seg, n):
    return jax.ops.segment_sum(src, seg, n)
kernel_name = 'mk_dlrm_tower_d1_rec_r8_c2f529'

def setup_inputs(seed: int=0):
    np.random.seed(seed)
    _w = jnp.asarray

    def _rec_inputs():
        import jax
        import jax.numpy as jnp
        _tk = jax.random.key(seed)
        dense_ctx = jax.random.normal(jax.random.fold_in(_tk, 190), (512, 16), jnp.float32)
        ids = jnp.stack([jax.random.randint(jax.random.fold_in(_tk, 200 + f), (512,), 0, v, jnp.int32) for f, v in enumerate([12500, 12500, 12500, 1000, 1250, 1000, 125000, 1000, 12500, 12500, 125000, 1000, 125000, 12500, 125000, 12500, 12500, 125000, 1250, 1250, 12500, 125000, 1000, 1000, 1250, 1250, 12500, 1250, 1000, 1250, 1250, 1000, 12500, 12500, 12500, 1000, 1250, 1000, 12500])], axis=1)
        tbl_0 = 0.05 * jax.random.normal(jax.random.fold_in(_tk, 500 + 0), (12500, 32), jnp.float32)
        tbl_1 = 0.05 * jax.random.normal(jax.random.fold_in(_tk, 500 + 1), (12500, 32), jnp.float32)
        tbl_2 = 0.05 * jax.random.normal(jax.random.fold_in(_tk, 500 + 2), (12500, 32), jnp.float32)
        tbl_3 = 0.05 * jax.random.normal(jax.random.fold_in(_tk, 500 + 3), (1000, 32), jnp.float32)
        tbl_4 = 0.05 * jax.random.normal(jax.random.fold_in(_tk, 500 + 4), (1250, 32), jnp.float32)
        tbl_5 = 0.05 * jax.random.normal(jax.random.fold_in(_tk, 500 + 5), (1000, 32), jnp.float32)
        tbl_6 = 0.05 * jax.random.normal(jax.random.fold_in(_tk, 500 + 6), (125000, 32), jnp.float32)
        tbl_7 = 0.05 * jax.random.normal(jax.random.fold_in(_tk, 500 + 7), (1000, 32), jnp.float32)
        tbl_8 = 0.05 * jax.random.normal(jax.random.fold_in(_tk, 500 + 8), (12500, 32), jnp.float32)
        tbl_9 = 0.05 * jax.random.normal(jax.random.fold_in(_tk, 500 + 9), (12500, 32), jnp.float32)
        tbl_10 = 0.05 * jax.random.normal(jax.random.fold_in(_tk, 500 + 10), (125000, 32), jnp.float32)
        tbl_11 = 0.05 * jax.random.normal(jax.random.fold_in(_tk, 500 + 11), (1000, 32), jnp.float32)
        tbl_12 = 0.05 * jax.random.normal(jax.random.fold_in(_tk, 500 + 12), (125000, 32), jnp.float32)
        tbl_13 = 0.05 * jax.random.normal(jax.random.fold_in(_tk, 500 + 13), (12500, 32), jnp.float32)
        tbl_14 = 0.05 * jax.random.normal(jax.random.fold_in(_tk, 500 + 14), (125000, 32), jnp.float32)
        tbl_15 = 0.05 * jax.random.normal(jax.random.fold_in(_tk, 500 + 15), (12500, 32), jnp.float32)
        tbl_16 = 0.05 * jax.random.normal(jax.random.fold_in(_tk, 500 + 16), (12500, 32), jnp.float32)
        tbl_17 = 0.05 * jax.random.normal(jax.random.fold_in(_tk, 500 + 17), (125000, 32), jnp.float32)
        tbl_18 = 0.05 * jax.random.normal(jax.random.fold_in(_tk, 500 + 18), (1250, 32), jnp.float32)
        tbl_19 = 0.05 * jax.random.normal(jax.random.fold_in(_tk, 500 + 19), (1250, 32), jnp.float32)
        tbl_20 = 0.05 * jax.random.normal(jax.random.fold_in(_tk, 500 + 20), (12500, 32), jnp.float32)
        tbl_21 = 0.05 * jax.random.normal(jax.random.fold_in(_tk, 500 + 21), (125000, 32), jnp.float32)
        tbl_22 = 0.05 * jax.random.normal(jax.random.fold_in(_tk, 500 + 22), (1000, 32), jnp.float32)
        tbl_23 = 0.05 * jax.random.normal(jax.random.fold_in(_tk, 500 + 23), (1000, 32), jnp.float32)
        tbl_24 = 0.05 * jax.random.normal(jax.random.fold_in(_tk, 500 + 24), (1250, 32), jnp.float32)
        tbl_25 = 0.05 * jax.random.normal(jax.random.fold_in(_tk, 500 + 25), (1250, 32), jnp.float32)
        tbl_26 = 0.05 * jax.random.normal(jax.random.fold_in(_tk, 500 + 26), (12500, 32), jnp.float32)
        tbl_27 = 0.05 * jax.random.normal(jax.random.fold_in(_tk, 500 + 27), (1250, 32), jnp.float32)
        tbl_28 = 0.05 * jax.random.normal(jax.random.fold_in(_tk, 500 + 28), (1000, 32), jnp.float32)
        tbl_29 = 0.05 * jax.random.normal(jax.random.fold_in(_tk, 500 + 29), (1250, 32), jnp.float32)
        tbl_30 = 0.05 * jax.random.normal(jax.random.fold_in(_tk, 500 + 30), (1250, 32), jnp.float32)
        tbl_31 = 0.05 * jax.random.normal(jax.random.fold_in(_tk, 500 + 31), (1000, 32), jnp.float32)
        tbl_32 = 0.05 * jax.random.normal(jax.random.fold_in(_tk, 500 + 32), (12500, 32), jnp.float32)
        tbl_33 = 0.05 * jax.random.normal(jax.random.fold_in(_tk, 500 + 33), (12500, 32), jnp.float32)
        tbl_34 = 0.05 * jax.random.normal(jax.random.fold_in(_tk, 500 + 34), (12500, 32), jnp.float32)
        tbl_35 = 0.05 * jax.random.normal(jax.random.fold_in(_tk, 500 + 35), (1000, 32), jnp.float32)
        tbl_36 = 0.05 * jax.random.normal(jax.random.fold_in(_tk, 500 + 36), (1250, 32), jnp.float32)
        tbl_37 = 0.05 * jax.random.normal(jax.random.fold_in(_tk, 500 + 37), (1000, 32), jnp.float32)
        tbl_38 = 0.05 * jax.random.normal(jax.random.fold_in(_tk, 500 + 38), (12500, 32), jnp.float32)
        _rk = jax.random.fold_in(_tk, 7)
        W_top1 = 0.049029 * jax.random.normal(jax.random.fold_in(_tk, 801), (416, 512), jnp.float32)
        W_top2 = 0.0441942 * jax.random.normal(jax.random.fold_in(_tk, 802), (512, 256), jnp.float32)
        W_top3 = 0.0625 * jax.random.normal(jax.random.fold_in(_tk, 803), (256, 1), jnp.float32)
        b_top1 = jnp.zeros((512,), jnp.float32)
        b_top2 = jnp.zeros((256,), jnp.float32)
        return (dense_ctx, ids, tbl_0, tbl_1, tbl_2, tbl_3, tbl_4, tbl_5, tbl_6, tbl_7, tbl_8, tbl_9, tbl_10, tbl_11, tbl_12, tbl_13, tbl_14, tbl_15, tbl_16, tbl_17, tbl_18, tbl_19, tbl_20, tbl_21, tbl_22, tbl_23, tbl_24, tbl_25, tbl_26, tbl_27, tbl_28, tbl_29, tbl_30, tbl_31, tbl_32, tbl_33, tbl_34, tbl_35, tbl_36, tbl_37, tbl_38, W_top1, b_top1, W_top2, b_top2, W_top3)
    dense_ctx, ids, tbl_0, tbl_1, tbl_2, tbl_3, tbl_4, tbl_5, tbl_6, tbl_7, tbl_8, tbl_9, tbl_10, tbl_11, tbl_12, tbl_13, tbl_14, tbl_15, tbl_16, tbl_17, tbl_18, tbl_19, tbl_20, tbl_21, tbl_22, tbl_23, tbl_24, tbl_25, tbl_26, tbl_27, tbl_28, tbl_29, tbl_30, tbl_31, tbl_32, tbl_33, tbl_34, tbl_35, tbl_36, tbl_37, tbl_38, W_top1, b_top1, W_top2, b_top2, W_top3 = _rec_inputs()

    def _L0_rec_setup():
        import jax, jax.numpy as jnp
        import numpy as np
        LAYER_SIZE = [200, 200, 200]
        SPLIT_HALF = True
        key = jax.random.key(seed)
        ks = jax.random.split(key, 8)
        B, F0, D = (256, 39, 32)
        field_nums = [F0]
        for i, s in enumerate(LAYER_SIZE):
            field_nums.append(s // 2 if SPLIT_HALF and i != len(LAYER_SIZE) - 1 else s)
        inp = {'x': jax.random.normal(ks[0], (B, F0, D), dtype=jnp.float32)}
        for i, s in enumerate(LAYER_SIZE):
            fan_in = field_nums[i] * F0
            scale = float(np.sqrt(6.0 / (fan_in + s)))
            inp[f'W{i}'] = jax.random.uniform(ks[1 + i], (fan_in, s), dtype=jnp.float32, minval=-scale, maxval=scale)
            inp[f'b{i}'] = jnp.zeros((s,), dtype=jnp.float32)
        return inp
    _L0_rec_all = _L0_rec_setup()
    _L0_rec_in = {k: v for k, v in _L0_rec_all.items() if k in ('W0', 'W1', 'W2', 'b0', 'b1', 'b2')}
    del _L0_rec_all
    return {'dense_ctx': dense_ctx, 'ids': ids, 'tbl_0': tbl_0, 'tbl_1': tbl_1, 'tbl_2': tbl_2, 'tbl_3': tbl_3, 'tbl_4': tbl_4, 'tbl_5': tbl_5, 'tbl_6': tbl_6, 'tbl_7': tbl_7, 'tbl_8': tbl_8, 'tbl_9': tbl_9, 'tbl_10': tbl_10, 'tbl_11': tbl_11, 'tbl_12': tbl_12, 'tbl_13': tbl_13, 'tbl_14': tbl_14, 'tbl_15': tbl_15, 'tbl_16': tbl_16, 'tbl_17': tbl_17, 'tbl_18': tbl_18, 'tbl_19': tbl_19, 'tbl_20': tbl_20, 'tbl_21': tbl_21, 'tbl_22': tbl_22, 'tbl_23': tbl_23, 'tbl_24': tbl_24, 'tbl_25': tbl_25, 'tbl_26': tbl_26, 'tbl_27': tbl_27, 'tbl_28': tbl_28, 'tbl_29': tbl_29, 'tbl_30': tbl_30, 'tbl_31': tbl_31, 'tbl_32': tbl_32, 'tbl_33': tbl_33, 'tbl_34': tbl_34, 'tbl_35': tbl_35, 'tbl_36': tbl_36, 'tbl_37': tbl_37, 'tbl_38': tbl_38, 'W_top1': W_top1, 'b_top1': b_top1, 'W_top2': W_top2, 'b_top2': b_top2, 'W_top3': W_top3, 'L0_rec_W0': _L0_rec_in['W0'], 'L0_rec_W1': _L0_rec_in['W1'], 'L0_rec_W2': _L0_rec_in['W2'], 'L0_rec_b0': _L0_rec_in['b0'], 'L0_rec_b1': _L0_rec_in['b1'], 'L0_rec_b2': _L0_rec_in['b2']}

def reference(dense_ctx, ids, tbl_0, tbl_1, tbl_2, tbl_3, tbl_4, tbl_5, tbl_6, tbl_7, tbl_8, tbl_9, tbl_10, tbl_11, tbl_12, tbl_13, tbl_14, tbl_15, tbl_16, tbl_17, tbl_18, tbl_19, tbl_20, tbl_21, tbl_22, tbl_23, tbl_24, tbl_25, tbl_26, tbl_27, tbl_28, tbl_29, tbl_30, tbl_31, tbl_32, tbl_33, tbl_34, tbl_35, tbl_36, tbl_37, tbl_38, W_top1, b_top1, W_top2, b_top2, W_top3, L0_rec_W0, L0_rec_W1, L0_rec_W2, L0_rec_b0, L0_rec_b1, L0_rec_b2):
    import jax
    import jax.numpy as jnp

    def _L0_rec_ref(x, W0, W1, W2, b0, b1, b2):
        import jax, jax.numpy as jnp
        import numpy as np
        LAYER_SIZE = [200, 200, 200]
        SPLIT_HALF = True
        Ws = [W0, W1, W2]
        bs = [b0, b1, b2]
        B, F0, D = x.shape
        hidden = x
        finals = []
        n_layers = len(LAYER_SIZE)
        for i in range(n_layers):
            z = jnp.einsum('bmd,bnd->bmnd', x, hidden).reshape(B, -1, D)
            cur = jnp.einsum('bcd,co->bod', z, Ws[i]) + bs[i][None, :, None]
            cur = jax.nn.relu(cur)
            if SPLIT_HALF and i != n_layers - 1:
                half = LAYER_SIZE[i] // 2
                hidden, direct = (cur[:, :half, :], cur[:, half:, :])
            else:
                direct = cur
                hidden = cur
            finals.append(direct)
        result = jnp.concatenate(finals, axis=1)
        return jnp.sum(result, axis=-1)
    e = jnp.stack([tbl_0[ids[:, 0]], tbl_1[ids[:, 1]], tbl_2[ids[:, 2]], tbl_3[ids[:, 3]], tbl_4[ids[:, 4]], tbl_5[ids[:, 5]], tbl_6[ids[:, 6]], tbl_7[ids[:, 7]], tbl_8[ids[:, 8]], tbl_9[ids[:, 9]], tbl_10[ids[:, 10]], tbl_11[ids[:, 11]], tbl_12[ids[:, 12]], tbl_13[ids[:, 13]], tbl_14[ids[:, 14]], tbl_15[ids[:, 15]], tbl_16[ids[:, 16]], tbl_17[ids[:, 17]], tbl_18[ids[:, 18]], tbl_19[ids[:, 19]], tbl_20[ids[:, 20]], tbl_21[ids[:, 21]], tbl_22[ids[:, 22]], tbl_23[ids[:, 23]], tbl_24[ids[:, 24]], tbl_25[ids[:, 25]], tbl_26[ids[:, 26]], tbl_27[ids[:, 27]], tbl_28[ids[:, 28]], tbl_29[ids[:, 29]], tbl_30[ids[:, 30]], tbl_31[ids[:, 31]], tbl_32[ids[:, 32]], tbl_33[ids[:, 33]], tbl_34[ids[:, 34]], tbl_35[ids[:, 35]], tbl_36[ids[:, 36]], tbl_37[ids[:, 37]], tbl_38[ids[:, 38]]], axis=1)
    z = _L0_rec_ref(e, L0_rec_W0, L0_rec_W1, L0_rec_W2, L0_rec_b0, L0_rec_b1, L0_rec_b2)
    z = z.reshape(z.shape[0], -1)
    h = jnp.concatenate([z, dense_ctx], axis=1)
    h = jnp.maximum(h @ W_top1 + b_top1, 0.0)
    h = jnp.maximum(h @ W_top2 + b_top2, 0.0)
    y = h @ W_top3
    return y

_drawn_inputs = setup_inputs


def setup_inputs(seed=0):
    import zlib

    import numpy as np

    out = dict(_drawn_inputs(seed))
    spreads = {'b_top1': (0.0, 2.0),
     'b_top2': (0.0, 2.0),
     'L0_rec_b0': (0.0, 0.612),
     'L0_rec_b1': (0.0, 0.8),
     'L0_rec_b2': (0.0, 2.0)}
    factors = {'tbl_0': 8.0,
     'tbl_1': 8.0,
     'tbl_2': 8.0,
     'tbl_3': 8.0,
     'tbl_4': 8.0,
     'tbl_5': 8.0,
     'tbl_6': 8.0,
     'tbl_7': 8.0,
     'tbl_8': 8.0,
     'tbl_9': 8.0,
     'tbl_10': 8.0,
     'tbl_11': 8.0,
     'tbl_12': 8.0,
     'tbl_13': 8.0,
     'tbl_14': 8.0,
     'tbl_15': 8.0,
     'tbl_16': 8.0,
     'tbl_17': 8.0,
     'tbl_18': 8.0,
     'tbl_19': 8.0,
     'tbl_20': 8.0,
     'tbl_21': 8.0,
     'tbl_22': 8.0,
     'tbl_23': 8.0,
     'tbl_24': 8.0,
     'tbl_25': 8.0,
     'tbl_26': 8.0,
     'tbl_27': 8.0,
     'tbl_28': 8.0,
     'tbl_29': 8.0,
     'tbl_30': 8.0,
     'tbl_31': 8.0,
     'tbl_32': 8.0,
     'tbl_33': 8.0,
     'tbl_34': 8.0,
     'tbl_35': 8.0,
     'tbl_36': 8.0,
     'tbl_37': 8.0,
     'tbl_38': 8.0,
     'L0_rec_W0': 8.0,
     'L0_rec_W1': 7.239,
     'L0_rec_W2': 4.642,
     'dense_ctx': 32.074}
    for name, (base, spread) in spreads.items():
        noise = np.random.default_rng([zlib.crc32(name.encode()), seed]).standard_normal(out[name].shape)
        drawn = base * np.exp(spread * noise) if base else spread * noise
        out[name] = jnp.asarray(drawn.astype(out[name].dtype))
    for name, factor in factors.items():
        out[name] = (out[name] * factor).astype(out[name].dtype)
    return out
```

```python
from contextlib import ExitStack

import concourse.bass as bass
from concourse import mybir

F32 = mybir.dt.float32
F32R = mybir.dt.float32r
I32 = mybir.dt.int32
U32 = mybir.dt.uint32
ALU = mybir.AluOpType
ACT = mybir.ActivationFunctionType
AX = mybir.AxisListType

BATCH, FIELDS, DIM = 512, 39, 32
HIDDEN, MIX = 100, 200
CONTEXT, TOP1, TOP2 = 16, 512, 256
P = 128

GROUPS, FIELD_TILES = 5, 8
LANES, HIDDEN_TILES = 25, 4
ROWS = GROUPS * LANES
CHUNK_BATCH = 16
CHUNK = CHUNK_BATCH * DIM
CHUNKS = BATCH // CHUNK_BATCH
CHUNKS_PER_GATHER = P // CHUNK_BATCH

UNIT = 2
UNITS_OF_LAYER = [FIELD_TILES // UNIT, FIELD_TILES * HIDDEN_TILES // UNIT, FIELD_TILES * HIDDEN_TILES // UNIT]
UNITS_PER_STEP = sum(UNITS_OF_LAYER)
PASSES_PER_STEP = 3
PRODUCT_SLOTS = 2
SPLIT_SLOTS = 3
assert UNITS_PER_STEP % PRODUCT_SLOTS == 0 and UNITS_PER_STEP % SPLIT_SLOTS == 0


def pair_runs():
    runs = []
    for g in range(GROUPS):
        for lane in range(3 * FIELD_TILES):
            field = FIELD_TILES * ((g + lane // FIELD_TILES) % GROUPS) + lane % FIELD_TILES
            p = g * LANES + lane
            if field >= FIELDS:
                continue
            if runs and runs[-1][0] + runs[-1][2] == p and runs[-1][1] + runs[-1][2] == field:
                runs[-1][2] += 1
            else:
                runs.append([p, field, 1])
    return runs


PAIR_RUNS = pair_runs()


class Pass:

    def __init__(self, layer, ahead, first_unit, index):
        self.layer = layer
        self.ahead = ahead
        self.first_unit = first_unit
        self.index = index
        self.units = UNITS_OF_LAYER[layer]


OPENING = Pass(0, 0, 0, 0)


def passes_of_step(last):
    first = [Pass(1, 0, UNITS_OF_LAYER[0], 1)]
    if not last:
        first.append(Pass(0, 1, first[-1].first_unit + first[-1].units, 2))
    return first + [Pass(2, 0, first[-1].first_unit + first[-1].units, first[-1].index + 1)]


def following(p, last):
    if p is None:
        return None, False
    ps = passes_of_step(last)
    at = [q.index for q in ps].index(p.index)
    if at + 1 < len(ps):
        return ps[at + 1], False
    return (None, False) if last else (Pass(1, 1, UNITS_OF_LAYER[0] + UNITS_PER_STEP, 1 + PASSES_PER_STEP), True)


def tower(nc, dense_t, ids, tables, w0, w0_mirror, w1, w2, cin_bias, w_top1, b_top1, w_top2, b_top2, w_top3, out):
    with ExitStack() as whole:
        def sb(stack, name, shape, dt=F32):
            return stack.enter_context(nc.sbuf_tensor(name, shape, dt))

        def sem(name):
            return whole.enter_context(nc.semaphore(name))

        x_rows = nc.dram_tensor("x_rows", (CHUNKS, FIELDS, CHUNK), F32, kind="Internal").ap()

        w_hi, w_lo = [], []
        for layer, tiles in enumerate([(1,), (HIDDEN_TILES,), (HIDDEN_TILES,)]):
            w_hi.append(sb(whole, f"w{layer}_hi", [P, tiles[0], FIELD_TILES, MIX], F32R))
            w_lo.append(sb(whole, f"w{layer}_lo", [P, tiles[0], FIELD_TILES, MIX], F32R))
        mixed = sb(whole, "mixed", [P, 4, BATCH])
        sums = sb(whole, "sums", [P, 4, CHUNK_BATCH])
        bias = sb(whole, "bias", [P, 3, 2])
        bias_top1 = sb(whole, "bias_top1", [P, TOP1 // P])
        bias_top2 = sb(whole, "bias_top2", [P, TOP2 // P])
        y_row = sb(whole, "y_row", [P, BATCH])
        gather_ids = sb(whole, "gather_ids", [P, FIELDS], I32)
        gathered = sb(whole, "gathered", [P, FIELDS, DIM])

        with ExitStack() as opening:
            raw0 = sb(opening, "raw0", [P, 1, FIELD_TILES, MIX])
            raw0m = sb(opening, "raw0m", [P, 1, FIELD_TILES, MIX])
            raw1 = sb(opening, "raw1", [P, HIDDEN_TILES, FIELD_TILES, MIX])
            raw2 = sb(opening, "raw2", [P, HIDDEN_TILES, FIELD_TILES, MIX])
        raw = [raw0, raw1, raw2]

        with ExitStack() as main:
            fields = [sb(main, f"fields{n}", [P, FIELD_TILES, CHUNK]) for n in range(2)]
            pair = sb(main, "pair", [P, CHUNK])
            hidden = [None] + [sb(main, f"hidden{n}", [P, HIDDEN_TILES, CHUNK]) for n in (1, 2)]
            activated = [sb(main, f"activated{n}", [P, CHUNK]) for n in (0, 1)]
            z_hi = [sb(main, f"z_hi{n}", [P, UNIT, CHUNK], F32R) for n in range(SPLIT_SLOTS)]
            z_lo = [sb(main, f"z_lo{n}", [P, UNIT, CHUNK], F32R) for n in range(SPLIT_SLOTS)]

        closing = whole.enter_context(ExitStack())
        top1 = sb(closing, "top1", [P, 4, TOP1])
        top1_context = sb(closing, "top1_context", [P, TOP1])
        context = sb(closing, "context", [P, BATCH])
        top2 = sb(closing, "top2", [P, TOP1 // P, TOP2])
        top3 = sb(closing, "top3", [P, TOP2 // P])
        t1 = sb(closing, "t1", [P, TOP1 // P, BATCH])
        t2 = sb(closing, "t2", [P, TOP2 // P, BATCH])

        z = [whole.enter_context(nc.psum_tensor(f"z{n}", [P, UNIT, CHUNK], F32)) for n in range(PRODUCT_SLOTS)]
        mix = [whole.enter_context(nc.psum_tensor(f"mix{n}", [P, 2, CHUNK], F32)) for n in range(2)]

        raw_loaded = [sem(f"raw_loaded{n}") for n in range(4)]
        small_loaded = sem("small_loaded")
        w0_folded = sem("w0_folded")
        w_hi_made = sem("w_hi_made")
        w_lo_made = sem("w_lo_made")
        padding_zero = sem("padding_zero")
        ids_loaded = sem("ids_loaded")
        rows_gathered = sem("rows_gathered")
        rows_stored = sem("rows_stored")
        chunks_stored = sem("chunks_stored")
        fields_loaded = [sem(f"fields_loaded{n}") for n in range(2)]
        pair_loaded = sem("pair_loaded")
        hidden_loaded = [None] + [[sem(f"hidden{n}_loaded{j}") for j in range(HIDDEN_TILES)] for n in (1, 2)]
        products_made = sem("products_made")
        hi_made = sem("hi_made")
        lo_made = sem("lo_made")
        units_mixed = sem("units_mixed")
        passes_activated = sem("passes_activated")
        hidden_activated = [sem(f"hidden_activated{n}") for n in (0, 1)]
        passes_summed = sem("passes_summed")
        sums_stored = [sem(f"sums_stored{n}") for n in range(3)]
        top_loaded = sem("top_loaded")
        t1_mixed, t1_made = sem("t1_mixed"), sem("t1_made")
        t2_mixed, t2_made = sem("t2_mixed"), sem("t2_made")
        y_mixed, y_made, y_stored = sem("y_mixed"), sem("y_made"), sem("y_stored")

        waits_passed = {"sp": sem("sp_waits_passed"), "pool": sem("pool_waits_passed")}

        block = whole.enter_context(nc.Block())

        def wait_alone(engine, name, semaphore, count):
            engine.wait_ge(semaphore, count)
            engine.sem_inc(waits_passed[name], 1)

        def over_steps(engine, step):
            step(0, 0, True, False)
            with engine.Fori(1, CHUNKS - 2, 2) as c:
                step(c, 1, False, False)
                step(c + 1, 0, False, False)
            step(CHUNKS - 1, 1, False, True)

        def direct_halves(layer):
            return [(0, 2), (1, 3)] if layer == 2 else [(1, layer)]

        @block.sync
        def _(sp):
            for n, (tile, source) in enumerate([(raw0, w0), (raw0m, w0_mirror), (raw1, w1), (raw2, w2)]):
                sp.dma_start(tile[0:ROWS], source).then_inc(raw_loaded[n], 16)
            sp.dma_start(bias[0:HIDDEN], cin_bias).then_inc(small_loaded, 16)
            sp.dma_start(bias_top1[:], b_top1).then_inc(small_loaded, 16)
            sp.dma_start(bias_top2[:], b_top2).then_inc(small_loaded, 16)

            def load_fields(c, parity):
                wait_alone(sp, "sp", chunks_stored, c + 1)
                for g in range(GROUPS):
                    n = min(FIELD_TILES, FIELDS - FIELD_TILES * g)
                    rows = x_rows[bass.ds(c, 1), FIELD_TILES * g:FIELD_TILES * g + n, :]
                    sp.dma_start(fields[parity][LANES * g:LANES * (g + 1), 0:n, :],
                                 rows.to_broadcast([LANES, n, CHUNK])).then_inc(fields_loaded[parity], 16)
                for p, f, n in PAIR_RUNS:
                    sp.dma_start(pair[p:p + n, :],
                                 x_rows[bass.ds(c, 1), f:f + n, :].rearrange("c f s -> (c f) s")).then_inc(pair_loaded, 16)

            def spread_hidden(layer, c):
                wait_alone(sp, "sp", hidden_activated[layer - 1], c + 1)
                for j in range(HIDDEN_TILES):
                    for g in range(GROUPS):
                        sp.dma_start(hidden[layer][LANES * g:LANES * (g + 1), j, :],
                                     activated[layer - 1][LANES * j:LANES * (j + 1), :]
                                     ).then_inc(hidden_loaded[layer][j], 16)

            def store_sums(layer, c, passes):
                wait_alone(sp, "sp", passes_summed, passes)
                k, n = direct_halves(layer)[0][1], len(direct_halves(layer))
                sp.dma_start(mixed[0:HIDDEN, k:k + n, bass.ds(c * CHUNK_BATCH, CHUNK_BATCH)],
                             sums[0:HIDDEN, k:k + n, :]).then_inc(sums_stored[layer], 16)

            sp.wait_ge(padding_zero, 3)
            load_fields(0, 0)
            spread_hidden(1, 0)

            def step(c, parity, first, last):
                if first:
                    store_sums(0, 0, 1)
                if not last:
                    if not first:
                        wait_alone(sp, "sp", products_made, c * UNITS_PER_STEP + UNITS_OF_LAYER[0])
                    load_fields(c + 1, 1 - parity)
                if not first:
                    store_sums(2, c - 1, c * PASSES_PER_STEP + 1)
                spread_hidden(2, c)
                store_sums(1, c, c * PASSES_PER_STEP + 2)
                if not last:
                    spread_hidden(1, c + 1)
                    store_sums(0, c + 1, c * PASSES_PER_STEP + 3)

            over_steps(sp, step)

            store_sums(2, CHUNKS - 1, CHUNKS * PASSES_PER_STEP)
            sp.wait_ge(y_made, 1)
            sp.dma_start(out, y_row[0:1, :]).then_inc(y_stored, 16)
            sp.wait_ge(y_stored, 16)

        @block.gpsimd
        def _(pool):
            with pool.Fori(0, BATCH // P) as part:
                pool.dma_start(gather_ids[:], ids[bass.ds(part * P, P), :]).then_inc(ids_loaded, 16)
                wait_alone(pool, "pool", ids_loaded, part * 16 + 16)
                for f in range(FIELDS):
                    pool.indirect_dma_start(
                        out=gathered[:, f, :], out_offset=None, in_=tables[f],
                        in_offset=bass.IndirectOffsetOnAxis(ap=gather_ids[:, f:f + 1].bitcast(U32), axis=0),
                    ).then_inc(rows_gathered, 16)
                wait_alone(pool, "pool", rows_gathered, part * (16 * FIELDS) + 16 * FIELDS)
                for k in range(CHUNKS_PER_GATHER):
                    pool.dma_start(
                        x_rows[bass.ds(part * CHUNKS_PER_GATHER + k, 1), :, :].rearrange(
                            "c f (b d) -> b (c f) d", d=DIM),
                        gathered[k * CHUNK_BATCH:(k + 1) * CHUNK_BATCH, :, :]).then_inc(rows_stored, 16)
                wait_alone(pool, "pool", rows_stored, part * (16 * CHUNKS_PER_GATHER) + 16 * CHUNKS_PER_GATHER)
                pool.sem_inc(chunks_stored, CHUNKS_PER_GATHER)

        @block.scalar
        def _(act):
            for layer in range(3):
                if layer == 0:
                    act.wait_ge(w0_folded, 1)
                else:
                    act.wait_ge(raw_loaded[layer + 1], 16)
                for j in range(1 if layer == 0 else HIDDEN_TILES):
                    act.activation(w_hi[layer][0:ROWS, j], raw[layer][0:ROWS, j], ACT.Copy).then_inc(w_hi_made, 1)
            act.wait_ge(small_loaded, 48)

            def make_hi(c, unit):
                u = c * UNITS_PER_STEP + unit
                act.wait_ge(products_made, u + 1)
                if not isinstance(u, int) or u >= SPLIT_SLOTS:
                    act.wait_ge(units_mixed, u + 1 - SPLIT_SLOTS)
                act.activation(z_hi[unit % SPLIT_SLOTS][0:ROWS], z[unit % PRODUCT_SLOTS][0:ROWS],
                               ACT.Copy).then_inc(hi_made, 1)

            def activate(c, p, set_):
                act.wait_ge(units_mixed, c * UNITS_PER_STEP + p.first_unit + p.units)
                if p.layer < 2:
                    act.activation(activated[p.layer][0:HIDDEN], mix[set_][0:HIDDEN, 0], ACT.Relu,
                                   bias=bias[0:HIDDEN, p.layer, 0:1]).then_inc(hidden_activated[p.layer], 1)
                else:
                    act.activation(mix[set_][0:HIDDEN, 0], mix[set_][0:HIDDEN, 0], ACT.Relu,
                                   bias=bias[0:HIDDEN, p.layer, 0:1])
                act.activation(mix[set_][0:HIDDEN, 1], mix[set_][0:HIDDEN, 1], ACT.Relu,
                               bias=bias[0:HIDDEN, p.layer, 1:2]).then_inc(passes_activated, 1)

            for unit in range(OPENING.units):
                make_hi(0, unit)
            activate(0, OPENING, 0)

            def step(c, parity, first, last):
                before = None if first else (c - 1, passes_of_step(False)[-1])
                for p in passes_of_step(last):
                    for n in range(p.units):
                        needs_it = last and p.layer == 2
                        if before and n == (0 if needs_it else SPLIT_SLOTS - 1):
                            activate(*before, (parity * PASSES_PER_STEP + p.index - 1) % 2)
                        make_hi(c, p.first_unit + n)
                    before = (c, p)

            over_steps(act, step)
            activate(CHUNKS - 1, passes_of_step(True)[-1], (PASSES_PER_STEP * CHUNKS - 1) % 2)

            act.wait_ge(products_made, CHUNKS * UNITS_PER_STEP)
            act.dma_start(top1[0:HIDDEN], w_top1[0:4 * HIDDEN, :].rearrange("(k p) n -> p k n", p=HIDDEN)
                          ).then_inc(top_loaded, 16)
            act.dma_start(top1_context[0:CONTEXT], w_top1[4 * HIDDEN:, :]).then_inc(top_loaded, 16)
            act.dma_start(context[0:CONTEXT], dense_t).then_inc(top_loaded, 16)
            act.dma_start(top2[:], w_top2.rearrange("(k p) n -> p k n", p=P)).then_inc(top_loaded, 16)
            act.dma_start(top3[:], w_top3).then_inc(top_loaded, 16)
            for m in range(TOP1 // P):
                act.wait_ge(t1_mixed, m + 1)
                act.activation(t1[:, m], mix[m // 2][:, m % 2], ACT.Relu, bias=bias_top1[:, m:m + 1]).then_inc(t1_made, 1)
            for m in range(TOP2 // P):
                act.wait_ge(t2_mixed, m + 1)
                act.activation(t2[:, m], z[0][:, m], ACT.Relu, bias=bias_top2[:, m:m + 1]).then_inc(t2_made, 1)
            act.wait_ge(y_mixed, 1)
            act.activation(y_row[0:1, :], z[1][0:1, 0], ACT.Copy).then_inc(y_made, 1)

        @block.vector
        def _(dve):
            dve.wait_ge(raw_loaded[0], 16)
            dve.wait_ge(raw_loaded[1], 16)
            dve.tensor_tensor(raw0[0:ROWS], raw0[0:ROWS], raw0m[0:ROWS], ALU.add).then_inc(w0_folded, 1)
            tiles = 0
            for layer in range(3):
                for j in range(1 if layer == 0 else HIDDEN_TILES):
                    tiles += 1
                    dve.wait_ge(w_hi_made, tiles)
                    dve.tensor_tensor(w_lo[layer][0:ROWS, j], raw[layer][0:ROWS, j],
                                      w_hi[layer][0:ROWS, j].bitcast(F32), ALU.subtract).then_inc(w_lo_made, 1)
            dve.wait_ge(w_lo_made, tiles)
            first_row = (FIELDS // FIELD_TILES) * LANES // 32 * 32
            for n in range(2):
                dve.memset(fields[n][first_row:P, FIELD_TILES - 1, :], 0.0).then_inc(padding_zero, 1)
            dve.memset(pair[:], 0.0).then_inc(padding_zero, 1)

            def make_products(c, p, n, parity):
                j, i = divmod(n * UNIT, FIELD_TILES)
                chunk = c + p.ahead
                if n == 0:
                    if p.layer == 0:
                        dve.wait_ge(pair_loaded, chunk * (16 * len(PAIR_RUNS)) + 16 * len(PAIR_RUNS))
                        dve.wait_ge(fields_loaded[parity], (chunk - parity) * (8 * GROUPS) + 16 * GROUPS)
                if p.layer == 0:
                    other = pair[0:ROWS, :]
                else:
                    if i == 0:
                        dve.wait_ge(hidden_loaded[p.layer][j], chunk * (16 * GROUPS) + 16 * GROUPS)
                    other = hidden[p.layer][0:ROWS, j, :]
                unit = p.first_unit + n
                u = c * UNITS_PER_STEP + unit
                if not isinstance(u, int) or u >= PRODUCT_SLOTS:
                    dve.wait_ge(lo_made, u + 1 - PRODUCT_SLOTS)
                dve.tensor_tensor(z[unit % PRODUCT_SLOTS][0:ROWS], fields[parity][0:ROWS, i:i + UNIT, :],
                                  other.unsqueeze(1).to_broadcast([ROWS, UNIT, CHUNK]),
                                  ALU.mult).then_inc(products_made, 1)

            def make_lo(c, unit):
                u = c * UNITS_PER_STEP + unit
                dve.wait_ge(hi_made, u + 1)
                if not isinstance(u, int) or u >= SPLIT_SLOTS:
                    dve.wait_ge(units_mixed, u + 1 - SPLIT_SLOTS)
                dve.tensor_tensor(z_lo[unit % SPLIT_SLOTS][0:ROWS], z[unit % PRODUCT_SLOTS][0:ROWS],
                                  z_hi[unit % SPLIT_SLOTS][0:ROWS].bitcast(F32), ALU.subtract).then_inc(lo_made, 1)

            def sum_columns(c, p, set_):
                chunk = c + p.ahead
                dve.wait_ge(passes_activated, c * PASSES_PER_STEP + p.index + 1)
                if not isinstance(chunk, int) or chunk > 0:
                    dve.wait_ge(sums_stored[p.layer], chunk * 16)
                for half, k in direct_halves(p.layer):
                    last = dve.tensor_reduce(sums[0:HIDDEN, k, :],
                                             mix[set_][0:HIDDEN, half].rearrange("p (b d) -> p b d", d=DIM),
                                             AX.X, ALU.add)
                last.then_inc(passes_summed, 1)

            def run(c, p, parity, after, after_parity, needs_it, before, set_):
                for n in range(p.units):
                    if n + 1 < p.units:
                        make_products(c, p, n + 1, parity)
                    elif after and not needs_it:
                        make_products(c, after, 0, after_parity)
                    make_lo(c, p.first_unit + n)
                    if before and n == SPLIT_SLOTS:
                        sum_columns(*before, set_)

            layer1 = passes_of_step(False)[0]
            make_products(0, OPENING, 0, 0)
            run(0, OPENING, 0, layer1, 0, True, None, 0)
            sum_columns(0, OPENING, 0)
            make_products(0, layer1, 0, 0)

            def step(c, parity, first, last):
                before = None if first else (c - 1, passes_of_step(False)[-1])
                for p in passes_of_step(last):
                    after, _ = following(p, last)
                    needs_it = last and p.layer == 1
                    run(c, p, (parity + p.ahead) % 2, after, after and (parity + after.ahead) % 2, needs_it,
                        before, (parity * PASSES_PER_STEP + p.index - 1) % 2)
                    if needs_it:
                        make_products(c, after, 0, parity)
                    before = (c, p)

            over_steps(dve, step)
            sum_columns(CHUNKS - 1, passes_of_step(True)[-1], (PASSES_PER_STEP * CHUNKS - 1) % 2)

        @block.tensor
        def _(pe):
            pe.wait_ge(w_lo_made, 1)

            def mix_pass(c, p, set_):
                if not isinstance(c, int) or c * PASSES_PER_STEP + p.index >= 2:
                    pe.wait_ge(passes_summed, c * PASSES_PER_STEP + p.index - 1)
                for n in range(p.units):
                    unit = p.first_unit + n
                    slot = unit % SPLIT_SLOTS
                    u = c * UNITS_PER_STEP + unit
                    for part, (z_part, w_parts) in enumerate([(z_hi, (w_hi, w_lo)), (z_lo, (w_hi,))]):
                        pe.wait_ge(hi_made if part == 0 else lo_made, u + 1)
                        for k in range(UNIT):
                            j, i = divmod(n * UNIT + k, FIELD_TILES)
                            for w in w_parts:
                                for half in range(2):
                                    mm = pe.matmul(mix[set_][0:HIDDEN, half],
                                                   w[p.layer][0:ROWS, j, i, HIDDEN * half:HIDDEN * (half + 1)],
                                                   z_part[slot][0:ROWS, k, :],
                                                   start=(n == 0 and part == 0 and k == 0 and w is w_hi),
                                                   stop=(n == p.units - 1 and part == 1 and k == UNIT - 1))
                    mm.then_inc(units_mixed, 1)

            mix_pass(0, OPENING, 0)
            pe.wait_ge(w_lo_made, 1 + 2 * HIDDEN_TILES)

            def step(c, parity, first, last):
                for p in passes_of_step(last):
                    mix_pass(c, p, (parity * PASSES_PER_STEP + p.index) % 2)

            over_steps(pe, step)

            pe.wait_ge(top_loaded, 16 * 5)
            for n in range(3):
                pe.wait_ge(sums_stored[n], 16 * CHUNKS)
            for m in range(TOP1 // P):
                columns = slice(P * m, P * (m + 1))
                pe.matmul(mix[m // 2][:, m % 2], top1_context[0:CONTEXT, columns], context[0:CONTEXT, :],
                          start=True, stop=False)
                for k in range(4):
                    mm = pe.matmul(mix[m // 2][:, m % 2], top1[0:HIDDEN, k, columns], mixed[0:HIDDEN, k, :],
                                   start=False, stop=(k == 3))
                mm.then_inc(t1_mixed, 1)
            for m in range(TOP2 // P):
                for k in range(TOP1 // P):
                    if m == 0:
                        pe.wait_ge(t1_made, k + 1)
                    mm = pe.matmul(z[0][:, m], top2[:, k, P * m:P * (m + 1)], t1[:, k], start=(k == 0),
                                   stop=(k == TOP1 // P - 1))
                mm.then_inc(t2_mixed, 1)
            for k in range(TOP2 // P):
                pe.wait_ge(t2_made, k + 1)
                mm = pe.matmul(z[1][0:1, 0], top3[:, k:k + 1], t2[:, k], start=(k == 0), stop=(k == TOP2 // P - 1))
            mm.then_inc(y_mixed, 1)


def lay_out(inputs):
    import numpy as np

    pad = GROUPS * FIELD_TILES
    arrays = {"dense_t": np.ascontiguousarray(np.asarray(inputs["dense_ctx"]).T), "ids": np.asarray(inputs["ids"])}
    for f in range(FIELDS):
        arrays[f"tbl_{f}"] = np.asarray(inputs[f"tbl_{f}"])
    raw = np.asarray(inputs["L0_rec_W0"]).reshape(FIELDS, FIELDS, MIX)
    w0 = np.zeros((ROWS, 1, FIELD_TILES, MIX), raw.dtype)
    w0_mirror = np.zeros_like(w0)
    for g in range(GROUPS):
        m = slice(FIELD_TILES * g, min(FIELD_TILES * (g + 1), FIELDS))
        n_m = m.stop - m.start
        for turn in range(3):
            other = (g + turn) % GROUPS
            n = slice(FIELD_TILES * other, min(FIELD_TILES * (other + 1), FIELDS))
            p = g * LANES + turn * FIELD_TILES
            n_n = n.stop - n.start
            w0[p:p + n_n, 0, 0:n_m] = raw[m, n].transpose(1, 0, 2)
            if turn:
                w0_mirror[p:p + n_n, 0, 0:n_m] = raw[n, m]
    arrays["w0"], arrays["w0_mirror"] = w0, w0_mirror
    for layer in (1, 2):
        raw = np.asarray(inputs[f"L0_rec_W{layer}"]).reshape(FIELDS, HIDDEN, MIX)
        padded = np.zeros((pad, HIDDEN, MIX), raw.dtype)
        padded[:FIELDS] = raw
        tiled = padded.reshape(GROUPS, FIELD_TILES, HIDDEN_TILES, LANES, MIX).transpose(0, 3, 2, 1, 4)
        arrays[f"w{layer}"] = np.ascontiguousarray(tiled.reshape(ROWS, HIDDEN_TILES, FIELD_TILES, MIX))
    arrays["cin_bias"] = np.ascontiguousarray(
        np.stack([np.asarray(inputs[f"L0_rec_b{n}"]).reshape(2, HIDDEN).T for n in range(3)], axis=1))
    arrays["w_top1"] = np.asarray(inputs["W_top1"])
    arrays["b_top1"] = np.ascontiguousarray(np.asarray(inputs["b_top1"]).reshape(TOP1 // P, P).T)
    arrays["w_top2"] = np.asarray(inputs["W_top2"])
    arrays["b_top2"] = np.ascontiguousarray(np.asarray(inputs["b_top2"]).reshape(TOP2 // P, P).T)
    arrays["w_top3"] = np.ascontiguousarray(np.asarray(inputs["W_top3"]).reshape(TOP2 // P, P).T)
    return arrays


def kernel(**inputs):
    import concourse.bacc as bacc
    from concourse.bass_utils import run_bass_kernel_spmd

    nc = bacc.Bacc("TRN2", target_bir_lowering=False, num_devices=1)
    arrays = lay_out(inputs)
    aps = {name: nc.dram_tensor(name, a.shape, mybir.dt.from_np(a.dtype), kind="ExternalInput").ap()
           for name, a in arrays.items()}
    out = nc.dram_tensor("out", (BATCH, 1), F32, kind="ExternalOutput").ap()
    tables = [aps.pop(f"tbl_{f}") for f in range(FIELDS)]
    tower(nc, tables=tables, out=out.rearrange("b one -> one b"), **aps)
    result = run_bass_kernel_spmd(nc, [arrays], core_ids=[0])
    return result.results[0]["out"]
```

```python
from contextlib import ExitStack

import concourse.bass as bass
from concourse import mybir

F32 = mybir.dt.float32
F32R = mybir.dt.float32r
I32 = mybir.dt.int32
U32 = mybir.dt.uint32
ALU = mybir.AluOpType
ACT = mybir.ActivationFunctionType
AX = mybir.AxisListType

BATCH, FIELDS, DIM = 512, 39, 32
HIDDEN, MIX = 100, 200
CONTEXT, TOP1, TOP2 = 16, 512, 256
P = 128

GROUPS, FIELD_TILES = 5, 8
LANES, HIDDEN_TILES = 25, 4
ROWS = GROUPS * LANES
CHUNK_BATCH = 8
CHUNK = CHUNK_BATCH * DIM
CHUNKS = BATCH // CHUNK_BATCH
BLOCKS = CHUNK // P

GATHERS = 3
GATHER = FIELDS * CHUNK_BATCH // GATHERS
assert GATHER * GATHERS == FIELDS * CHUNK_BATCH and GATHER <= P

UNIT = 4
UNITS_OF_LAYER = [FIELD_TILES // UNIT, FIELD_TILES * HIDDEN_TILES // UNIT, FIELD_TILES * HIDDEN_TILES // UNIT]
UNITS_PER_STEP = sum(UNITS_OF_LAYER)
PASSES_PER_STEP = 3
WHOLE = {1: 3}
SPLIT_PER_STEP = UNITS_PER_STEP - len(WHOLE)
SLOTS = 3

ADD, SPREAD, TURN, ACTIVATE, SUM = SLOTS, SLOTS + 1, 3, SLOTS + 3, SLOTS + 4

ORDER = [(0, 0), (1, 0), (0, 1)]
for _c in range(1, CHUNKS - 1):
    ORDER += [(1, _c), (0, _c + 1), (2, _c - 1)]
ORDER += [(1, CHUNKS - 1), (2, CHUNKS - 2), (2, CHUNKS - 1)]
NUMBER = {p: n for n, p in enumerate(ORDER)}
IS_WHOLE = [WHOLE.get(layer) == n for layer, _ in ORDER for n in range(UNITS_OF_LAYER[layer])]
FIRST_UNIT = {p: sum(UNITS_OF_LAYER[q[0]] for q in ORDER[:n]) for n, p in enumerate(ORDER)}
LOOP_FIRST = 3


class Pass:

    def __init__(self, layer, chunk, like=None):
        self.layer, self.chunk = layer, chunk
        self.fixed = isinstance(chunk, int)
        self.like = chunk if self.fixed else like
        self.units = UNITS_OF_LAYER[layer]
        self.bank = 0 if self.fixed and (layer, chunk) == ORDER[-1] else layer

    def number(self, layer=None, back=0):
        layer = self.layer if layer is None else layer
        if self.fixed:
            return NUMBER[layer, self.chunk - back]
        return self.chunk * PASSES_PER_STEP + (NUMBER[layer, self.like - back] - self.like * PASSES_PER_STEP)

    def unit(self, n=0):
        first = FIRST_UNIT[self.layer, self.like] + n
        return first if self.fixed else self.chunk * UNITS_PER_STEP + (first - self.like * UNITS_PER_STEP)

    def whole(self, n):
        return WHOLE.get(self.layer) == n

    def split(self, n, fixed=False):
        first = IS_WHOLE[:FIRST_UNIT[self.layer, self.like] + n].count(False)
        return first if self.fixed or fixed else self.chunk * SPLIT_PER_STEP + (first - self.like * SPLIT_PER_STEP)

    def slot(self, n):
        return self.split(n, fixed=True) % SLOTS

    def before_in_slot(self, n):
        unit = FIRST_UNIT[self.layer, self.like] + n
        same = [u for u in range(unit) if IS_WHOLE[u] == self.whole(n)]
        places = 1 if self.whole(n) else SLOTS
        return None if len(same) < places else self.unit(n) + (same[-places] + 1 - unit)


def step_passes(c, like):
    return [Pass(1, c, like), Pass(0, c + 1, like + 1), Pass(2, c - 1, like - 1)]


class Segment:

    def __init__(self, passes, behind=(), ahead=None, fresh=False, weights=range(0)):
        self.passes, self.behind, self.ahead = passes, list(behind), ahead
        self.fresh, self.weights = fresh, weights

    def timeline(self):
        units = [(p, n) for p in self.passes for n in range(p.units)]
        ends, at = {}, 0
        for p in reversed(self.behind):
            at -= p.units
            ends[at + p.units - 1] = p
        at = 0
        for p in self.passes:
            at += p.units
            ends[at - 1] = p
        following = units[1:] + [(self.ahead, 0) if self.ahead else (None, 0)]
        steps = [(p, n, q, m) for (p, n), (q, m) in zip(units, following)]
        if not self.ahead:
            steps += [(None, 0, None, 0)] * SUM
        for k, (p, n, q, m) in enumerate(steps):
            yield p, n, q, m, {k - e: done for e, done in ends.items() if k > e}


def run_segments(engine, run):
    run(Segment([Pass(0, 0)], fresh=True, weights=PIECES_1))
    run(Segment([Pass(1, 0), Pass(0, 1)], fresh=True, weights=PIECES_2))
    run(Segment(step_passes(1, 1), (), Pass(1, 2), fresh=True))
    run(Segment(step_passes(2, 2), step_passes(1, 1), Pass(1, 3)))
    with engine.Fori(LOOP_FIRST, CHUNKS - 1 - (SLOTS - 1), SLOTS) as c:
        for s in range(SLOTS):
            like = LOOP_FIRST + s
            run(Segment(step_passes(c + s, like), step_passes(c + s - 1, like - 1), Pass(1, c + s + 1, like + 1)))
    last = CHUNKS - 1
    run(Segment([Pass(1, last), Pass(2, last - 1), Pass(2, last)], step_passes(last - 1, last - 1)))


def pair_runs():
    runs = []
    for g in range(GROUPS):
        for lane in range(3 * FIELD_TILES):
            field = FIELD_TILES * ((g + lane // FIELD_TILES) % GROUPS) + lane % FIELD_TILES
            p = g * LANES + lane
            if field >= FIELDS:
                continue
            if runs and runs[-1][0] + runs[-1][2] == p and runs[-1][1] + runs[-1][2] == field:
                runs[-1][2] += 1
            else:
                runs.append([p, field, 1])
    return runs


PAIR_RUNS = pair_runs()
PIECES = [(0, 0)] + [(layer, j) for layer in (1, 2) for j in range(HIDDEN_TILES)]
PIECES_1 = range(1, 1 + HIDDEN_TILES)
PIECES_2 = range(1 + HIDDEN_TILES, 1 + 2 * HIDDEN_TILES)


def raw_place(n):
    return (0, 1) if n == 0 else ((n - 1) % 2, 2 + (n - 1) // 2)


def piece_tiles(n):
    layer, j = PIECES[n]
    whole_tile = WHOLE[layer] * UNIT if layer in WHOLE else None
    first = FIELD_TILES * j
    if whole_tile is None or first + FIELD_TILES <= whole_tile:
        return slice(0, FIELD_TILES), slice(first, first + FIELD_TILES)
    if first < whole_tile:
        return slice(0, whole_tile - first), slice(first, whole_tile)
    return slice(0, FIELD_TILES), slice(first - UNIT, first - UNIT + FIELD_TILES)


assert FIELD_TILES == 2 * UNIT and 0 not in WHOLE and all(n % 2 for n in WHOLE.values())


def tower(nc, table, dense_t, ids, table_start, identity, w0, w0_mirror, w1, w2, bias_hidden, bias_direct,
          w_top1, b_top1, w_top2, b_top2, w_top3, out):
    with ExitStack() as whole:
        def sb(stack, name, shape, dt=F32):
            return stack.enter_context(nc.sbuf_tensor(name, shape, dt))

        def sem(name):
            return whole.enter_context(nc.semaphore(name))

        x_rows = nc.dram_tensor("x_rows", (CHUNKS, FIELDS, CHUNK), F32, kind="Internal").ap()

        w = [sb(whole, f"w{layer}_split", [P, (UNITS_OF_LAYER[layer] - (layer in WHOLE)) * UNIT, 2, MIX], F32R)
             for layer in range(3)]
        w_whole = sb(whole, "w_whole", [P, len(WHOLE), UNIT, MIX])
        mixed = sb(whole, "mixed", [P, 4, BATCH])
        sums = sb(whole, "sums", [P, 4, CHUNK_BATCH])
        hidden_bias = sb(whole, "hidden_bias", [P, 2, HIDDEN_TILES])
        direct_bias = sb(whole, "direct_bias", [P, 4])
        top1_bias = sb(whole, "top1_bias", [P, TOP1 // P])
        top2_bias = sb(whole, "top2_bias", [P, TOP2 // P])
        ident = sb(whole, "ident", [P, P])
        all_ids = sb(whole, "all_ids", [P, CHUNKS, GATHERS], I32)
        first_rows = sb(whole, "first_rows", [P, GATHERS], I32)
        rows_now = sb(whole, "rows_now", [P, GATHERS], I32)
        gathered = sb(whole, "gathered", [P, GATHERS, DIM])

        with ExitStack() as main:
            fields = [None] * SLOTS
            fields[1] = sb(main, "fields1", [P, FIELD_TILES, CHUNK])
            hidden1 = sb(main, "hidden1", [P, HIDDEN_TILES, CHUNK])
            fields[0] = sb(main, "fields0", [P, FIELD_TILES, CHUNK])
            pair = sb(main, "pair", [P, CHUNK])
            z = [sb(main, f"z{n}", [P, UNIT, CHUNK]) for n in range(SLOTS)]
            z_hi = [sb(main, f"z_hi{n}", [P, UNIT, CHUNK], F32R) for n in range(SLOTS)]
            z_lo = [sb(main, f"z_lo{n}", [P, UNIT, CHUNK], F32R) for n in range(SLOTS)]
            z_whole = sb(main, "z_whole", [P, UNIT, CHUNK])
            cross = sb(main, "cross", [P, BLOCKS, MIX])
            total = sb(main, "total", [P, BLOCKS, MIX])
            spread = sb(main, "spread", [P, BLOCKS, HIDDEN_TILES, ROWS])
            hidden2 = [sb(main, "hidden2_0", [P, HIDDEN_TILES, CHUNK])]
            with ExitStack() as opening:
                raw = [sb(opening, f"raw{n}", [P, FIELD_TILES, MIX]) for n in range(2)]
            fields[2] = sb(main, "fields2", [P, FIELD_TILES, CHUNK])
            hidden2 += [sb(main, f"hidden2_{n}", [P, HIDDEN_TILES, CHUNK]) for n in (1, 2)]

        closing = whole.enter_context(ExitStack())
        top1 = sb(closing, "top1", [P, 4, TOP1])
        top1_context = sb(closing, "top1_context", [P, TOP1])
        context = sb(closing, "context", [P, BATCH])
        top2 = sb(closing, "top2", [P, TOP1 // P, TOP2])
        top3 = sb(closing, "top3", [P, TOP2 // P])
        t1 = sb(closing, "t1", [P, TOP1 // P, BATCH])
        t2 = sb(closing, "t2", [P, TOP2 // P, BATCH])
        y_row = sb(closing, "y_row", [P, BATCH])

        mix = [whole.enter_context(nc.psum_tensor(f"mix{n}", [P, BLOCKS, 2 * CHUNK], F32)) for n in range(3)]
        direct = [whole.enter_context(nc.psum_tensor(f"direct{n}", [P, 2 * CHUNK], F32)) for n in range(2)]

        raw_loaded = [sem(f"raw_loaded{n}") for n in range(2)]
        w0_folded = sem("w0_folded")
        whole_loaded = sem("whole_loaded")
        w_hi_made = sem("w_hi_made")
        w_lo_made = sem("w_lo_made")
        small_loaded = sem("small_loaded")
        ids_loaded = sem("ids_loaded")
        padding_zero = sem("padding_zero")
        rows_made = sem("rows_made")
        rows_gathered = sem("rows_gathered")
        rows_stored = sem("rows_stored")
        fields_loaded = sem("fields_loaded")
        pair_loaded = sem("pair_loaded")
        products_made = sem("products_made")
        hi_made = sem("hi_made")
        lo_made = sem("lo_made")
        units_mixed = sem("units_mixed")
        cross_copied = sem("cross_copied")
        totals_made = sem("totals_made")
        totals_spread = sem("totals_spread")
        passes_turned = sem("passes_turned")
        passes_activated = sem("passes_activated")
        passes_summed = sem("passes_summed")
        sums_stored = [sem(f"sums_stored{n}") for n in range(3)]
        top_loaded = sem("top_loaded")
        t1_mixed, t1_made = sem("t1_mixed"), sem("t1_made")
        t2_mixed, t2_made = sem("t2_mixed"), sem("t2_made")
        y_mixed, y_made, y_stored = sem("y_mixed"), sem("y_made"), sem("y_stored")
        waits_passed = {"sp": sem("sp_waits_passed"), "pool": sem("pool_waits_passed")}

        block = whole.enter_context(nc.Block())

        def wait_alone(engine, name, semaphore, count):
            engine.wait_ge(semaphore, count)
            engine.sem_inc(waits_passed[name], 1)

        def direct_rows(layer):
            return slice(2, 4) if layer == 2 else slice(layer, layer + 1)

        def turned_direct(p):
            if p.layer == 2:
                return mix[p.bank][0:HIDDEN, 0, :].rearrange("p (h s) -> p h s", h=2)
            return direct[p.layer][0:HIDDEN, 0:CHUNK].unsqueeze(1)

        @block.sync
        def _(sp):
            def load_fields(c, like):
                wait_alone(sp, "sp", rows_stored, c * 16 + 16)
                for g in range(GROUPS):
                    n = min(FIELD_TILES, FIELDS - FIELD_TILES * g)
                    rows = x_rows[bass.ds(c, 1), FIELD_TILES * g:FIELD_TILES * g + n, :]
                    sp.dma_start(fields[like % SLOTS][LANES * g:LANES * (g + 1), 0:n, :],
                                 rows.to_broadcast([LANES, n, CHUNK])).then_inc(fields_loaded, 16)
                for p, f, n in PAIR_RUNS:
                    sp.dma_start(pair[p:p + n, :],
                                 x_rows[bass.ds(c, 1), f:f + n, :].rearrange("c f s -> (c f) s")
                                 ).then_inc(pair_loaded, 16)

            def store_sums(p):
                wait_alone(sp, "sp", passes_summed, p.number() + 1)
                sp.dma_start(mixed[0:HIDDEN, direct_rows(p.layer), bass.ds(p.chunk * CHUNK_BATCH, CHUNK_BATCH)],
                             sums[0:HIDDEN, direct_rows(p.layer), :]).then_inc(sums_stored[p.layer], 16)

            sp.dma_start(raw[0][0:ROWS], w0[:, 0]).then_inc(raw_loaded[0], 16)
            sp.dma_start(raw[1][0:ROWS], w0_mirror[:, 0]).then_inc(raw_loaded[1], 16)
            for k, layer in enumerate(WHOLE):
                j, half = divmod(WHOLE[layer], 2)
                source = (w1, w2)[layer - 1]
                sp.dma_start(w_whole[0:ROWS, k], source[:, j, UNIT * half:UNIT * (half + 1)]
                             ).then_inc(whole_loaded, 16)
            for tile, source in [(hidden_bias[0:ROWS], bias_hidden), (direct_bias[0:HIDDEN], bias_direct),
                                 (top1_bias[:], b_top1), (top2_bias[:], b_top2)]:
                sp.dma_start(tile, source).then_inc(small_loaded, 16)
            sp.dma_start(ident[:], identity).then_inc(small_loaded, 16)
            sp.wait_ge(padding_zero, 3)
            load_fields(0, 0)

            def load_raw(n):
                layer, j = PIECES[n]
                sp.wait_ge(w_lo_made, max(n - 1, 1))
                tiles, _ = piece_tiles(n)
                sp.dma_start(raw[raw_place(n)[0]][0:ROWS, tiles], (w1, w2)[layer - 1][:, j, tiles]
                             ).then_inc(raw_loaded[raw_place(n)[0]], 16)

            for n in PIECES_1:
                load_raw(n)
            sp.wait_ge(products_made, UNITS_OF_LAYER[0])
            load_fields(1, 1)

            def run(segment):
                for p in segment.passes:
                    if p.layer == 1 and (not p.fixed or 0 < p.chunk < CHUNKS - 1):
                        last_user = Pass(0, 1) if p.fixed and p.chunk == 1 else Pass(2, p.chunk - 2, p.like - 2)
                        wait_alone(sp, "sp", products_made, last_user.unit(last_user.units))
                        load_fields(p.chunk + 1, p.like + 1)
                for p in segment.behind[-1:] + (segment.passes[:-1] if segment.ahead else segment.passes):
                    store_sums(p)
                if segment.weights == PIECES_1:
                    load_raw(PIECES_2[0])
                    load_raw(PIECES_2[1])
                if segment.weights == PIECES_2:
                    load_raw(PIECES_2[2])
                    load_raw(PIECES_2[3])
                    sp.wait_ge(padding_zero, 4)

            run_segments(sp, run)
            sp.wait_ge(y_made, 1)
            sp.dma_start(out, y_row[0:1, :]).then_inc(y_stored, 16)
            sp.wait_ge(y_stored, 16)

        @block.gpsimd
        def _(pool):
            pool.wait_ge(ids_loaded, 32)
            with pool.Fori(0, CHUNKS) as c:
                pool.tensor_tensor(rows_now[0:GATHER, :],
                                   all_ids[0:GATHER, bass.ds(c, 1), :].rearrange("p c q -> p (c q)"),
                                   first_rows[0:GATHER, :], ALU.add).then_inc(rows_made, 1)
                wait_alone(pool, "pool", rows_made, c + 1)
                for q in range(GATHERS):
                    pool.indirect_dma_start(
                        out=gathered[0:GATHER, q, :], out_offset=None, in_=table,
                        in_offset=bass.IndirectOffsetOnAxis(ap=rows_now[0:GATHER, q:q + 1].bitcast(U32), axis=0),
                    ).then_inc(rows_gathered, 16)
                wait_alone(pool, "pool", rows_gathered, c * (16 * GATHERS) + 16 * GATHERS)
                pool.dma_start(x_rows[bass.ds(c, 1), :, :].rearrange("c f (b d) -> (c f b) d", d=DIM)
                               .rearrange("(q p) d -> p q d", p=GATHER),
                               gathered[0:GATHER]).then_inc(rows_stored, 16)
                wait_alone(pool, "pool", rows_stored, c * 16 + 16)

        @block.scalar
        def _(act):
            act.dma_start(all_ids[0:GATHER], ids).then_inc(ids_loaded, 16)
            act.dma_start(first_rows[0:GATHER], table_start).then_inc(ids_loaded, 16)

            def split_weights(pieces):
                for n in pieces:
                    buffer, loads = raw_place(n)
                    tiles, places = piece_tiles(n)
                    if n == 0:
                        act.wait_ge(w0_folded, 1)
                    else:
                        act.wait_ge(raw_loaded[buffer], 16 * loads)
                    act.activation(w[PIECES[n][0]][0:ROWS, places, 0, :], raw[buffer][0:ROWS, tiles], ACT.Copy
                                   ).then_inc(w_hi_made, 1)

            def make_hi(p, n):
                act.wait_ge(products_made, p.unit(n) + 1)
                if p.before_in_slot(n) is not None:
                    act.wait_ge(units_mixed, p.before_in_slot(n))
                act.activation(z_hi[p.slot(n)][0:ROWS], z[p.slot(n)][0:ROWS], ACT.Copy).then_inc(hi_made, 1)

            def copy_cross(p):
                act.wait_ge(units_mixed, p.unit(p.units))
                act.activation(cross[:], mix[p.bank][:, :, MIX:2 * MIX], ACT.Copy).then_inc(cross_copied, 1)

            def spread_total(p):
                act.wait_ge(totals_made, p.number() + 1)
                for b in range(BLOCKS):
                    lanes = total[:, b, 0:HIDDEN].rearrange("p (j l) -> p j l", j=HIDDEN_TILES).unsqueeze(2)
                    last = act.activation(spread[:, b].rearrange("p j (g l) -> p j g l", g=GROUPS),
                                          lanes.to_broadcast([P, HIDDEN_TILES, GROUPS, LANES]), ACT.Copy)
                last.then_inc(totals_spread, 1)

            def activate(p):
                act.wait_ge(passes_turned, p.number() + 1)
                if p.layer < 2:
                    tiles = hidden1 if p.layer == 0 else hidden2[p.like % SLOTS]
                    for j in range(HIDDEN_TILES):
                        act.activation(tiles[0:ROWS, j, :],
                                       mix[p.bank][0:ROWS, j // 2, CHUNK * (j % 2):CHUNK * (j % 2 + 1)], ACT.Relu,
                                       bias=hidden_bias[0:ROWS, p.layer, j:j + 1])
                rows = direct_rows(p.layer)
                turned = turned_direct(p)
                for half, k in enumerate(range(rows.start, rows.stop)):
                    last = act.activation(turned[:, half], turned[:, half], ACT.Relu,
                                          bias=direct_bias[0:HIDDEN, k:k + 1])
                last.then_inc(passes_activated, 1)

            def run(segment):
                for p, n, _, _, ended in segment.timeline():
                    if ACTIVATE in ended:
                        activate(ended[ACTIVATE])
                    if ADD in ended:
                        copy_cross(ended[ADD])
                    if SPREAD in ended and ended[SPREAD].layer < 2:
                        spread_total(ended[SPREAD])
                    if p and not p.whole(n):
                        make_hi(p, n)
                split_weights(segment.weights)

            split_weights(range(1))
            act.wait_ge(small_loaded, 16 * 5)
            run_segments(act, run)

            act.wait_ge(products_made, CHUNKS * UNITS_PER_STEP)
            act.dma_start(top1[0:HIDDEN], w_top1[0:4 * HIDDEN, :].rearrange("(k p) n -> p k n", p=HIDDEN)
                          ).then_inc(top_loaded, 16)
            act.dma_start(top1_context[0:CONTEXT], w_top1[4 * HIDDEN:, :]).then_inc(top_loaded, 16)
            act.dma_start(context[0:CONTEXT], dense_t).then_inc(top_loaded, 16)
            act.dma_start(top2[:], w_top2.rearrange("(k p) n -> p k n", p=P)).then_inc(top_loaded, 16)
            act.dma_start(top3[:], w_top3).then_inc(top_loaded, 16)
            for m in range(TOP1 // P):
                act.wait_ge(t1_mixed, m + 1)
                act.activation(t1[:, m], mix[m // 2][:, m % 2], ACT.Relu, bias=top1_bias[:, m:m + 1]).then_inc(t1_made, 1)
            for m in range(TOP2 // P):
                act.wait_ge(t2_mixed, m + 1)
                act.activation(t2[:, m], mix[2][:, m], ACT.Relu, bias=top2_bias[:, m:m + 1]).then_inc(t2_made, 1)
            act.wait_ge(y_mixed, 1)
            act.activation(y_row[0:1, :], direct[0][0:1, :], ACT.Copy).then_inc(y_made, 1)

        @block.vector
        def _(dve):
            first_row = (FIELDS // FIELD_TILES) * LANES // 32 * 32
            dve.memset(pair[:], 0.0).then_inc(padding_zero, 1)
            for n in range(2):
                dve.memset(fields[n][first_row:P, FIELD_TILES - 1, :], 0.0).then_inc(padding_zero, 1)
            dve.wait_ge(raw_loaded[0], 16)
            dve.wait_ge(raw_loaded[1], 16)
            dve.tensor_tensor(raw[0][0:ROWS], raw[0][0:ROWS], raw[1][0:ROWS], ALU.add).then_inc(w0_folded, 1)

            def split_weights(pieces):
                for n in pieces:
                    split = w[PIECES[n][0]]
                    tiles, places = piece_tiles(n)
                    dve.wait_ge(w_hi_made, n + 1)
                    dve.tensor_tensor(split[0:ROWS, places, 1, :], raw[raw_place(n)[0]][0:ROWS, tiles],
                                      split[0:ROWS, places, 0, :].bitcast(F32), ALU.subtract).then_inc(w_lo_made, 1)

            def make_products(p, n):
                j, i = divmod(n * UNIT, FIELD_TILES)
                if p.layer == 0:
                    if n == 0:
                        dve.wait_ge(pair_loaded, p.chunk * (16 * len(PAIR_RUNS)) + 16 * len(PAIR_RUNS))
                        dve.wait_ge(fields_loaded, p.chunk * (16 * GROUPS) + 16 * GROUPS)
                    other = pair[0:ROWS, :]
                else:
                    if n == 0:
                        dve.wait_ge(passes_activated, p.number(p.layer - 1) + 1)
                    other = (hidden1 if p.layer == 1 else hidden2[p.like % SLOTS])[0:ROWS, j, :]
                if p.whole(n):
                    if p.before_in_slot(n) is not None:
                        dve.wait_ge(units_mixed, p.before_in_slot(n))
                elif not p.fixed or p.split(n) >= SLOTS:
                    dve.wait_ge(lo_made, p.split(n) + 1 - SLOTS)
                place = z_whole if p.whole(n) else z[p.slot(n)]
                dve.tensor_tensor(place[0:ROWS], fields[p.like % SLOTS][0:ROWS, i:i + UNIT, :],
                                  other.unsqueeze(1).to_broadcast([ROWS, UNIT, CHUNK]),
                                  ALU.mult).then_inc(products_made, 1)

            def make_lo(p, n):
                dve.wait_ge(hi_made, p.split(n) + 1)
                if p.before_in_slot(n) is not None:
                    dve.wait_ge(units_mixed, p.before_in_slot(n))
                dve.tensor_tensor(z_lo[p.slot(n)][0:ROWS], z[p.slot(n)][0:ROWS],
                                  z_hi[p.slot(n)][0:ROWS].bitcast(F32), ALU.subtract).then_inc(lo_made, 1)

            def add_cross(p):
                dve.wait_ge(cross_copied, p.number() + 1)
                if not p.fixed or p.number() > 0:
                    dve.wait_ge(passes_turned, p.number())
                dve.tensor_tensor(total[:], mix[p.bank][:, :, 0:MIX], cross[:], ALU.add).then_inc(totals_made, 1)

            def sum_columns(p):
                dve.wait_ge(passes_activated, p.number() + 1)
                if not p.fixed or p.chunk > 0:
                    dve.wait_ge(sums_stored[p.layer], p.chunk * 16)
                dve.tensor_reduce(sums[0:HIDDEN, direct_rows(p.layer), :],
                                  turned_direct(p).rearrange("p h (b d) -> p h b d", d=DIM),
                                  AX.X, ALU.add).then_inc(passes_summed, 1)

            def run(segment):
                if segment.fresh:
                    make_products(segment.passes[0], 0)
                for p, n, q, m, ended in segment.timeline():
                    if q:
                        make_products(q, m)
                    if ADD in ended:
                        add_cross(ended[ADD])
                    if SUM in ended:
                        sum_columns(ended[SUM])
                    if p and not p.whole(n):
                        make_lo(p, n)
                split_weights(segment.weights)
                if segment.weights == PIECES_2:
                    dve.wait_ge(w_lo_made, len(PIECES))
                    dve.memset(fields[2][first_row:P, FIELD_TILES - 1, :], 0.0).then_inc(padding_zero, 1)

            split_weights(range(1))
            run_segments(dve, run)

        @block.tensor
        def _(pe):
            def mix_unit(p, n):
                if n == 0:
                    if p.fixed:
                        pe.wait_ge(w_lo_made, 1 if p.layer == 0 else len(PIECES) if p.layer == 2 else 2)
                    if not p.fixed or p.chunk > 0:
                        banks_last = p.number(back=1) if p.bank == p.layer else p.number(layer=p.bank)
                        pe.wait_ge(passes_summed, banks_last + 1)
                if p.fixed and (p.layer, p.chunk) == (1, 0) and n % 2 == 0:
                    pe.wait_ge(w_lo_made, 2 + n // 2)
                if p.whole(n):
                    pe.wait_ge(products_made, p.unit(n) + 1)
                    if p.fixed:
                        pe.wait_ge(whole_loaded, 16 * len(WHOLE))
                    for k in range(UNIT):
                        for b in range(BLOCKS):
                            mm = pe.matmul(mix[p.bank][:, b, 0:MIX], z_whole[0:ROWS, k, P * b:P * (b + 1)],
                                           w_whole[0:ROWS, list(WHOLE).index(p.layer), k, :], start=False,
                                           stop=(n == p.units - 1 and k == UNIT - 1), skip_group_check=True)
                    mm.then_inc(units_mixed, 1)
                    return
                first = n * UNIT - (UNIT if n > WHOLE.get(p.layer, n) else 0)
                for made, part, columns in ((hi_made, z_hi, 2), (lo_made, z_lo, 1)):
                    pe.wait_ge(made, p.split(n) + 1)
                    for k in range(UNIT):
                        for b in range(BLOCKS):
                            mm = pe.matmul(mix[p.bank][:, b, 0:columns * MIX],
                                           part[p.slot(n)][0:ROWS, k, P * b:P * (b + 1)],
                                           w[p.layer][0:ROWS, first + k, 0:columns, :].rearrange("p c n -> p (c n)"),
                                           start=(n == 0 and k == 0 and part is z_hi),
                                           stop=(n == p.units - 1 and k == UNIT - 1 and part is z_lo),
                                           skip_group_check=True)
                mm.then_inc(units_mixed, 1)

            def hidden_passes(p):
                before = sum(q[0] < 2 for q in ORDER[:NUMBER[p.layer, p.like]])
                return before if p.fixed else p.chunk * 2 + (before - 2 * p.like)

            def turn(p):
                if p.layer < 2:
                    pe.wait_ge(totals_spread, hidden_passes(p) + 1)
                else:
                    pe.wait_ge(totals_made, p.number() + 1)
                for b in range(BLOCKS):
                    if p.layer < 2:
                        for j in range(HIDDEN_TILES):
                            at = CHUNK * (j % 2) + P * b
                            pe.transpose(mix[p.bank][0:ROWS, j // 2, at:at + P], spread[:, b, j, :], ident[:])
                    halves = range(2) if p.layer == 2 else (1,)
                    for h, half in enumerate(halves):
                        last = pe.transpose(turned_direct(p)[:, h, P * b:P * (b + 1)],
                                            total[:, b, HIDDEN * half:HIDDEN * (half + 1)], ident[:])
                last.then_inc(passes_turned, 1)

            def run(segment):
                for p, n, _, _, ended in segment.timeline():
                    if TURN in ended:
                        turn(ended[TURN])
                    if p:
                        mix_unit(p, n)

            pe.wait_ge(small_loaded, 16 * 5)
            run_segments(pe, run)

            pe.wait_ge(top_loaded, 16 * 5)
            for n in range(3):
                pe.wait_ge(sums_stored[n], 16 * CHUNKS)
            for m in range(TOP1 // P):
                columns = slice(P * m, P * (m + 1))
                pe.matmul(mix[m // 2][:, m % 2], top1_context[0:CONTEXT, columns], context[0:CONTEXT, :],
                          start=True, stop=False)
                for k in range(4):
                    mm = pe.matmul(mix[m // 2][:, m % 2], top1[0:HIDDEN, k, columns], mixed[0:HIDDEN, k, :],
                                   start=False, stop=(k == 3))
                mm.then_inc(t1_mixed, 1)
            for m in range(TOP2 // P):
                for k in range(TOP1 // P):
                    if m == 0:
                        pe.wait_ge(t1_made, k + 1)
                    mm = pe.matmul(mix[2][:, m], top2[:, k, P * m:P * (m + 1)], t1[:, k], start=(k == 0),
                                   stop=(k == TOP1 // P - 1))
                mm.then_inc(t2_mixed, 1)
            for k in range(TOP2 // P):
                pe.wait_ge(t2_made, k + 1)
                mm = pe.matmul(direct[0][0:1, :], top3[:, k:k + 1], t2[:, k], start=(k == 0), stop=(k == TOP2 // P - 1))
            mm.then_inc(y_mixed, 1)


def lay_out(inputs):
    import numpy as np

    def given(name):
        return np.asarray(inputs[name])

    tables = [given(f"tbl_{f}") for f in range(FIELDS)]
    starts = np.cumsum([0] + [t.shape[0] for t in tables[:-1]]).astype(np.int32)
    by_row = np.repeat(starts, CHUNK_BATCH).reshape(GATHERS, GATHER)
    by_chunk = given("ids").reshape(CHUNKS, CHUNK_BATCH, FIELDS).transpose(0, 2, 1).reshape(CHUNKS, GATHERS, GATHER)
    arrays = {
        "table": np.concatenate(tables),
        "dense_t": np.ascontiguousarray(given("dense_ctx").T),
        "ids": np.ascontiguousarray(by_chunk.transpose(2, 0, 1)),
        "table_start": np.ascontiguousarray(by_row.T),
        "identity": np.eye(P, dtype=np.float32),
    }
    raw = given("L0_rec_W0").reshape(FIELDS, FIELDS, MIX)
    w0 = np.zeros((ROWS, 1, FIELD_TILES, MIX), raw.dtype)
    w0_mirror = np.zeros_like(w0)
    for g in range(GROUPS):
        m = slice(FIELD_TILES * g, min(FIELD_TILES * (g + 1), FIELDS))
        for turn in range(3):
            other = (g + turn) % GROUPS
            n = slice(FIELD_TILES * other, min(FIELD_TILES * (other + 1), FIELDS))
            p = g * LANES + turn * FIELD_TILES
            rows = slice(p, p + n.stop - n.start)
            w0[rows, 0, 0:m.stop - m.start] = raw[m, n].transpose(1, 0, 2)
            if turn:
                w0_mirror[rows, 0, 0:m.stop - m.start] = raw[n, m]
    arrays["w0"], arrays["w0_mirror"] = w0, w0_mirror
    for layer in (1, 2):
        raw = given(f"L0_rec_W{layer}").reshape(FIELDS, HIDDEN, MIX)
        padded = np.zeros((GROUPS * FIELD_TILES, HIDDEN, MIX), raw.dtype)
        padded[:FIELDS] = raw
        tiled = padded.reshape(GROUPS, FIELD_TILES, HIDDEN_TILES, LANES, MIX).transpose(0, 3, 2, 1, 4)
        arrays[f"w{layer}"] = np.ascontiguousarray(tiled.reshape(ROWS, HIDDEN_TILES, FIELD_TILES, MIX))
    biases = [given(f"L0_rec_b{n}") for n in range(3)]
    by_lane = np.stack([b[:HIDDEN].reshape(HIDDEN_TILES, LANES).T for b in biases[:2]], axis=1)
    arrays["bias_hidden"] = np.ascontiguousarray(np.tile(by_lane, (GROUPS, 1, 1)))
    arrays["bias_direct"] = np.ascontiguousarray(
        np.stack([biases[0][HIDDEN:], biases[1][HIDDEN:], biases[2][:HIDDEN], biases[2][HIDDEN:]], axis=1))
    arrays["w_top1"] = given("W_top1")
    arrays["b_top1"] = np.ascontiguousarray(given("b_top1").reshape(TOP1 // P, P).T)
    arrays["w_top2"] = given("W_top2")
    arrays["b_top2"] = np.ascontiguousarray(given("b_top2").reshape(TOP2 // P, P).T)
    arrays["w_top3"] = np.ascontiguousarray(given("W_top3").reshape(TOP2 // P, P).T)
    return arrays


def kernel(**inputs):
    import concourse.bacc as bacc
    from concourse.bass_utils import run_bass_kernel_spmd

    nc = bacc.Bacc("TRN2", target_bir_lowering=False, num_devices=1)
    arrays = lay_out(inputs)
    aps = {name: nc.dram_tensor(name, a.shape, mybir.dt.from_np(a.dtype), kind="ExternalInput").ap()
           for name, a in arrays.items()}
    out = nc.dram_tensor("out", (BATCH, 1), F32, kind="ExternalOutput").ap()
    tower(nc, out=out.rearrange("b one -> one b"), **aps)
    result = run_bass_kernel_spmd(nc, [arrays], core_ids=[0])
    return result.results[0]["out"]
```

```python
from contextlib import ExitStack

import concourse.bass as bass
from concourse import mybir

F32 = mybir.dt.float32
F32R = mybir.dt.float32r
I32 = mybir.dt.int32
U32 = mybir.dt.uint32
ALU = mybir.AluOpType
ACT = mybir.ActivationFunctionType

BATCH, FIELDS, DIM = 512, 39, 32
HIDDEN, MIX = 100, 200
CONTEXT, TOP1, TOP2 = 16, 512, 256
TOP1_ROWS = HIDDEN + CONTEXT // 4
P = 128

GROUPS, FIELD_TILES = 5, 8
LANES, HIDDEN_TILES = 25, 4
ROWS = GROUPS * LANES
CHUNK_BATCH = 8
CHUNK = CHUNK_BATCH * DIM
CHUNKS = BATCH // CHUNK_BATCH
BLOCKS = CHUNK // P

GATHERS = 3
GATHER = FIELDS * CHUNK_BATCH // GATHERS
assert GATHER * GATHERS == FIELDS * CHUNK_BATCH and GATHER <= P

DISTANCES = FIELDS // 2 + 1
TURNS = 3
PARTNER_TILES = (DISTANCES + TURNS - 1) // TURNS
PAIR_ROWS = TURNS * FIELDS
REPEATED = TURNS * PARTNER_TILES - 1
ROW_STORES = 3
PAIR_LOADS = 3
assert FIELDS % 2 == 1 and PAIR_ROWS <= P and FIELDS + REPEATED >= GROUPS * FIELD_TILES

UNIT = 4
TILES_OF_LAYER = [PARTNER_TILES, FIELD_TILES * HIDDEN_TILES, FIELD_TILES * HIDDEN_TILES]
ROWS_OF_LAYER = [PAIR_ROWS, ROWS, ROWS]
UNITS_OF_LAYER = [(tiles + UNIT - 1) // UNIT for tiles in TILES_OF_LAYER]
UNITS_PER_STEP = sum(UNITS_OF_LAYER)
PASSES_PER_STEP = 3
WHOLE = {1: 3}
SPLIT_PER_STEP = UNITS_PER_STEP - len(WHOLE)
SLOTS = 3

ADD, TURN, ACTIVATE = SLOTS, 3, SLOTS + 3
DIRECT_HALVES = [(1,), (1,), (0, 1)]
SUM_BATCH = 4
FINISHED = ACTIVATE + 2 * CHUNK_BATCH // SUM_BATCH


def sums_at(p, distance):
    parts = [(half, b) for half in DIRECT_HALVES[p.layer] for b in range(0, CHUNK_BATCH, SUM_BATCH)]
    k = distance - ACTIVATE - (p.layer < 2)
    return parts[k:k + 1] if k >= 0 else []


LAYER0_AFTER = 5
STEP = [(1, 0, 0, LAYER0_AFTER), (0, 1, 0, UNITS_OF_LAYER[0]), (1, 0, LAYER0_AFTER, UNITS_OF_LAYER[1]),
        (2, -1, 0, UNITS_OF_LAYER[2])]
OPENING = [(0, 0), (0, 1), (1, 0)]
CLOSING = [(1, CHUNKS - 1), (2, CHUNKS - 2), (2, CHUNKS - 1)]


def whole_passes(passes):
    return [(layer, chunk, n) for layer, chunk in passes for n in range(UNITS_OF_LAYER[layer])]


SCHEDULE = whole_passes(OPENING) + [(layer, step + ahead, n) for step in range(1, CHUNKS - 1)
                                    for layer, ahead, first, end in STEP for n in range(first, end)]
SCHEDULE += whole_passes(CLOSING)
POSITION = {unit: k for k, unit in enumerate(SCHEDULE)}
IS_WHOLE = [WHOLE.get(layer) == n for layer, _, n in SCHEDULE]
ORDER = [(layer, chunk) for layer, chunk, n in SCHEDULE if n == UNITS_OF_LAYER[layer] - 1]
NUMBER = {p: n for n, p in enumerate(ORDER)}
LOOP_FIRST = 3


def tiles_in(layer, n):
    return min(UNIT, TILES_OF_LAYER[layer] - UNIT * n)


def bank_of(layer, chunk):
    return {(0, 1): 3, (1, 0): 2, (2, CHUNKS - 1): 3}.get((layer, chunk), layer)


class Pass:

    def __init__(self, layer, chunk, like=None):
        self.layer, self.chunk = layer, chunk
        self.fixed = isinstance(chunk, int)
        self.like = chunk if self.fixed else like
        self.units = UNITS_OF_LAYER[layer]
        self.bank = bank_of(layer, chunk) if self.fixed else layer

    def number(self, back=0):
        if self.fixed:
            return NUMBER[self.layer, self.chunk - back]
        return self.chunk * PASSES_PER_STEP + (NUMBER[self.layer, self.like - back] - self.like * PASSES_PER_STEP)

    def before_in_banks(self):
        if not self.fixed:
            return self.number(back=1) + 1
        start = POSITION[self.layer, self.chunk, 0]
        before = [n + 1 for n, p in enumerate(ORDER) if bank_of(*p) == self.bank and POSITION[(*p, 0)] < start]
        return before[-1] if before else None

    def unit(self, n=0):
        first = POSITION[self.layer, self.like, n]
        return first if self.fixed else self.chunk * UNITS_PER_STEP + (first - self.like * UNITS_PER_STEP)

    def all_units(self):
        return self.unit(self.units - 1) + 1

    def whole(self, n):
        return WHOLE.get(self.layer) == n

    def split(self, n, fixed=False):
        first = IS_WHOLE[:POSITION[self.layer, self.like, n]].count(False)
        return first if self.fixed or fixed else self.chunk * SPLIT_PER_STEP + (first - self.like * SPLIT_PER_STEP)

    def slot(self, n):
        return self.split(n, fixed=True) % SLOTS

    def before_in_slot(self, n):
        unit = POSITION[self.layer, self.like, n]
        same = [u for u in range(unit) if IS_WHOLE[u] == self.whole(n)]
        places = 1 if self.whole(n) else SLOTS
        return None if len(same) < places else self.unit(n) + (same[-places] + 1 - unit)


class Run:

    def __init__(self, p, first, end):
        self.p, self.first, self.end = p, first, end

    def ends_pass(self):
        return self.p is not None and self.end == self.p.units


def all_of(layer, chunk):
    return Run(Pass(layer, chunk), 0, UNITS_OF_LAYER[layer])


def step_runs(c, like):
    passes = {layer: Pass(layer, c + ahead, like + ahead) for layer, ahead, _, _ in STEP}
    return [Run(passes[layer], first, end) for layer, _, first, end in STEP]


class Segment:

    def __init__(self, runs, behind=(), ahead=None, fresh=False, pieces=None):
        self.runs, self.behind, self.ahead = runs, list(behind), ahead
        self.fresh, self.pieces = fresh, pieces or {}

    def timeline(self):
        ends, at = {}, -sum(r.end - r.first for r in self.behind)
        for r in self.behind + self.runs:
            at += r.end - r.first
            if r.ends_pass():
                ends[at - 1] = r.p
        units = [(r.p, n) for r in self.runs for n in range(r.first, r.end)]
        following = units[1:] + [(self.ahead, 0) if self.ahead else (None, 0)]
        steps = [(p, n, q, m) for (p, n), (q, m) in zip(units, following)]
        if not self.ahead:
            steps += [(None, 0, None, 0)] * FINISHED
        for k, (p, n, q, m) in enumerate(steps):
            yield p, n, q, m, {k - e: done for e, done in ends.items() if k > e}, self.pieces.get(k, ())


def run_segments(engine, run):
    first, second, third = [all_of(*p) for p in OPENING]
    opening = [first, Run(None, 0, ACTIVATE - 1), second, third]
    run(Segment(opening, (), Pass(1, 1), fresh=True, pieces=PIECES_AFTER))
    run(Segment(step_runs(1, 1), opening, Pass(1, 2)))
    run(Segment(step_runs(2, 2), step_runs(1, 1), Pass(1, 3)))
    with engine.Fori(LOOP_FIRST, CHUNKS - 1 - (SLOTS - 1), SLOTS) as c:
        for s in range(SLOTS):
            like = LOOP_FIRST + s
            run(Segment(step_runs(c + s, like), step_runs(c + s - 1, like - 1), Pass(1, c + s + 1, like + 1)))
    run(Segment([all_of(*p) for p in CLOSING], step_runs(CHUNKS - 2, CHUNKS - 2)))


PIECES = [(layer, n) for layer in range(3) for n in range(UNITS_OF_LAYER[layer]) if WHOLE.get(layer) != n]
RAWS = 3
PIECES_BEFORE = range(0, 5)
PIECES_AFTER = {1: range(5, 9), 4: range(9, 11), 5: range(11, 12), 7: range(12, 13), 8: range(13, 14),
                9: range(14, 15), 10: range(15, 16), 11: range(16, len(PIECES))}


def split_places(layer, n):
    first = UNIT * (n - (n > WHOLE.get(layer, n)))
    return slice(first, first + tiles_in(layer, n))


def tower(nc, table, context_t, ids, identity, w0, w0_mirror, w1, w2, biases,
          w_top1, b_top1, w_top2, b_top2, w_top3, out):
    with ExitStack() as whole:
        def sb(stack, name, shape, dt=F32):
            return stack.enter_context(nc.sbuf_tensor(name, shape, dt))

        def sem(name):
            return whole.enter_context(nc.semaphore(name))

        x_rows = nc.dram_tensor("x_rows", (CHUNKS, FIELDS + REPEATED, CHUNK), F32, kind="Internal").ap()
        hidden_rows = [nc.dram_tensor(f"hidden_rows{n}", (HIDDEN, CHUNK), F32, kind="Internal").ap() for n in range(2)]

        w = [sb(whole, f"w{layer}_split", [P, TILES_OF_LAYER[layer] - (layer in WHOLE) * UNIT, 2, MIX], F32R)
             for layer in range(3)]
        w_whole = sb(whole, "w_whole", [P, len(WHOLE), UNIT, MIX])
        mixed = sb(whole, "mixed", [P, 4, BATCH])
        bias = sb(whole, "bias", [P, 3, 2])
        top1_bias = sb(whole, "top1_bias", [P, TOP1 // P])
        top2_bias = sb(whole, "top2_bias", [P, TOP2 // P])
        ident = sb(whole, "ident", [P, P])
        all_ids = sb(whole, "all_ids", [P, CHUNKS + 1, GATHERS], I32)
        rows_now = sb(whole, "rows_now", [P, GATHERS], I32)
        gathered = sb(whole, "gathered", [P, GATHERS, DIM])

        with ExitStack() as main:
            fields = [None] * SLOTS
            fields[1] = sb(main, "fields1", [P, FIELD_TILES, CHUNK])
            hidden1 = sb(main, "hidden1", [P, HIDDEN_TILES, CHUNK])
            fields[0] = sb(main, "fields0", [P, FIELD_TILES, CHUNK])
            single = sb(main, "single", [P, CHUNK])
            partners = sb(main, "partners", [P, PARTNER_TILES - UNIT, CHUNK])
            z = [sb(main, f"z{n}", [P, UNIT, CHUNK]) for n in range(SLOTS)]
            z_hi = [sb(main, f"z_hi{n}", [P, UNIT, CHUNK], F32R) for n in range(SLOTS)]
            z_lo = [sb(main, f"z_lo{n}", [P, UNIT, CHUNK], F32R) for n in range(SLOTS)]
            z_whole = sb(main, "z_whole", [P, UNIT, CHUNK])
            cross = sb(main, "cross", [P, BLOCKS, MIX])
            total = sb(main, "total", [P, BLOCKS, MIX])
            hidden_out = [sb(main, f"hidden_out{n}", [P, CHUNK]) for n in range(2)]
            hidden2 = [sb(main, "hidden2_0", [P, HIDDEN_TILES, CHUNK])]
            with ExitStack() as opening:
                raw = [sb(opening, f"raw{n}", [P, UNIT, MIX]) for n in range(RAWS)]
            mirror = [z[n + 1][:, :, 0:MIX] for n in range(UNITS_OF_LAYER[0])]
            fields[2] = sb(main, "fields2", [P, FIELD_TILES, CHUNK])
            hidden2 += [sb(main, f"hidden2_{n}", [P, HIDDEN_TILES, CHUNK]) for n in (1, 2)]

        closing = whole.enter_context(ExitStack())
        top1 = sb(closing, "top1", [P, 4, TOP1])
        top2 = sb(closing, "top2", [P, TOP1 // P, TOP2])
        top3 = sb(closing, "top3", [P, TOP2 // P])
        t1 = sb(closing, "t1", [P, TOP1 // P, BATCH])
        t2 = sb(closing, "t2", [P, TOP2 // P, BATCH])
        y_row = sb(closing, "y_row", [P, BATCH])

        mix = [whole.enter_context(nc.psum_tensor(f"mix{n}", [P, BLOCKS, 2 * CHUNK], F32)) for n in range(4)]

        raw_loaded = [sem(f"raw_loaded{n}") for n in range(RAWS)]
        mirror_loaded = sem("mirror_loaded")
        w0_folded = sem("w0_folded")
        whole_loaded = sem("whole_loaded")
        w_hi_made = sem("w_hi_made")
        w_lo_made = sem("w_lo_made")
        small_loaded = sem("small_loaded")
        ids_loaded = sem("ids_loaded")
        rows_made = sem("rows_made")
        rows_gathered = sem("rows_gathered")
        rows_stored = sem("rows_stored")
        fields_loaded = sem("fields_loaded")
        pairs_loaded = sem("pairs_loaded")
        products_made = sem("products_made")
        hi_made = sem("hi_made")
        lo_made = sem("lo_made")
        units_mixed = sem("units_mixed")
        cross_copied = sem("cross_copied")
        totals_made = sem("totals_made")
        passes_turned = sem("passes_turned")
        passes_summed = sem("passes_summed")
        hidden_activated = [sem(f"hidden_activated{n}") for n in range(2)]
        hidden_stored = [sem(f"hidden_stored{n}") for n in range(2)]
        hidden_loaded = [sem(f"hidden_loaded{n}") for n in range(2)]
        top1_loaded, top23_loaded = sem("top1_loaded"), sem("top23_loaded")
        t1_mixed, t1_made = sem("t1_mixed"), sem("t1_made")
        t2_mixed, t2_made = sem("t2_mixed"), sem("t2_made")
        y_mixed, y_made, y_stored = sem("y_mixed"), sem("y_made"), sem("y_stored")
        waits_passed = {"sp": sem("sp_waits_passed"), "pool": sem("pool_waits_passed")}

        block = whole.enter_context(nc.Block())

        def wait_alone(engine, name, semaphore, count):
            engine.wait_ge(semaphore, count)
            engine.sem_inc(waits_passed[name], 1)

        def hidden_of(p):
            if p.layer == 1:
                return hidden2[p.like % SLOTS]
            return hidden2[2] if p.fixed and p.chunk == 0 else hidden1

        def partner_tiles(c, like):
            return hidden2[0 if isinstance(c, int) and c == 1 else like % SLOTS], partners

        def unit_area(p, n):
            return slice(0, ROWS_OF_LAYER[p.layer]), slice(0, tiles_in(p.layer, n))

        def turned(p):
            return mix[p.bank][0:HIDDEN, :, 0:CHUNK]

        def t1_bank(m):
            return mix[m // 2][:, m % 2]

        @block.sync
        def _(sp):
            def load_fields(c, like):
                rows = x_rows[bass.ds(c, 1), 0:GROUPS * FIELD_TILES, :]
                rows = rows.rearrange("c (g i) s -> (c g) (i s)", i=FIELD_TILES)
                sp.dma_start(fields[like % SLOTS][0:ROWS].rearrange("p i s -> p (i s)"),
                             rows.unsqueeze(1).to_broadcast([GROUPS, LANES, FIELD_TILES * CHUNK])
                             ).then_inc(fields_loaded, 16)

            def load_pairs(c, like):
                wait_alone(sp, "sp", rows_stored, c * (16 * ROW_STORES) + 16 * ROW_STORES)
                sp.dma_start(single[0:PAIR_ROWS, :],
                             x_rows[bass.ds(c, 1), 0:FIELDS, :].to_broadcast([TURNS, FIELDS, CHUNK])
                             ).then_inc(pairs_loaded, 16)
                for n, tiles in enumerate(partner_tiles(c, like)):
                    count = tiles_in(0, n)
                    first = x_rows[bass.ds(c, 1), UNIT * n:UNIT * n + count, :]
                    source = bass.AP(tensor=first.tensor, offset=first.offset,
                                     ap=[[PARTNER_TILES * CHUNK, TURNS], [CHUNK, FIELDS], [1, count * CHUNK]])
                    sp.dma_start(tiles[0:PAIR_ROWS].rearrange("p i s -> p (i s)"), source).then_inc(pairs_loaded, 16)

            def move_hidden(p, last_user):
                wait_alone(sp, "sp", hidden_activated[p.layer], p.chunk + 1)
                if last_user:
                    wait_alone(sp, "sp", products_made, last_user.all_units())
                if not p.fixed or p.chunk > 0:
                    wait_alone(sp, "sp", hidden_loaded[p.layer], p.chunk * 16)
                sp.dma_start(hidden_rows[p.layer], hidden_out[p.layer][0:HIDDEN, :]
                             ).then_inc(hidden_stored[p.layer], 16)
                wait_alone(sp, "sp", hidden_stored[p.layer], p.chunk * 16 + 16)
                rows = hidden_rows[p.layer].rearrange("(l j) s -> l (j s)", j=HIDDEN_TILES)
                sp.dma_start(hidden_of(p)[0:ROWS].rearrange("p j s -> p (j s)"),
                             rows.unsqueeze(0).to_broadcast([GROUPS, LANES, HIDDEN_TILES * CHUNK])
                             ).then_inc(hidden_loaded[p.layer], 16)

            def load_raw(n):
                layer, unit = PIECES[n]
                if n >= RAWS:
                    sp.wait_ge(w_lo_made, n + 1 - RAWS)
                tiles = slice(UNIT * unit, UNIT * unit + tiles_in(layer, unit))
                sp.dma_start(raw[n % RAWS][0:ROWS_OF_LAYER[layer], 0:tiles_in(layer, unit)],
                             (w0, w1, w2)[layer][:, tiles]).then_inc(raw_loaded[n % RAWS], 16)

            sp.dma_start(all_ids[0:GATHER], ids).then_inc(ids_loaded, 16)
            for n in range(UNITS_OF_LAYER[0]):
                load_raw(n)
                sp.dma_start(mirror[n][0:PAIR_ROWS, 0:tiles_in(0, n)], w0_mirror[:, UNIT * n:UNIT * n + tiles_in(0, n)]
                             ).then_inc(mirror_loaded, 16)
            load_raw(2)
            for k, layer in enumerate(WHOLE):
                sp.dma_start(w_whole[0:ROWS, k], (w0, w1, w2)[layer][:, UNIT * WHOLE[layer]:UNIT * WHOLE[layer] + UNIT]
                             ).then_inc(whole_loaded, 16)
            for tile, source in [(bias[0:HIDDEN], biases), (top1_bias[:], b_top1), (top2_bias[:], b_top2),
                                 (ident[:], identity), (mixed[HIDDEN:TOP1_ROWS], context_t)]:
                sp.dma_start(tile, source).then_inc(small_loaded, 16)
            for n in range(UNITS_OF_LAYER[0] + 1, 5):
                load_raw(n)
            load_pairs(0, 0)
            for n in range(5, 12):
                load_raw(n)
            sp.wait_ge(products_made, UNITS_OF_LAYER[0])
            load_pairs(1, 1)
            load_fields(0, 0)
            load_raw(12)

            def run(segment):
                step = segment.runs[0].p
                if step.layer == 1 and segment.ahead:
                    last_user = Pass(1, 0) if step.fixed and step.chunk == 1 else Pass(2, step.chunk - 2, step.like - 2)
                    wait_alone(sp, "sp", products_made, last_user.all_units())
                    load_pairs(step.chunk + 1, step.like + 1)
                    load_fields(step.chunk + 1, step.like + 1)
                ended = [r.p for r in segment.behind[-1:] + segment.runs[:-1] if r.ends_pass()]
                for p in ended:
                    if p.layer < 2:
                        move_hidden(p, step if p.layer == 0 and step.layer == 1 else None)
                    if p.fixed and (p.layer, p.chunk) == (0, 0):
                        for n in range(13, len(PIECES)):
                            load_raw(n)
                        sp.wait_ge(products_made, Pass(1, 0).unit() + 1)
                        load_fields(1, 1)
                if segment.pieces:
                    sp.wait_ge(w_lo_made, len(PIECES))
                if not segment.ahead:
                    sp.wait_ge(products_made, step.all_units())
                    sp.dma_start(top1[0:TOP1_ROWS], w_top1).then_inc(top1_loaded, 16)

            run_segments(sp, run)
            sp.wait_ge(y_made, 1)
            sp.dma_start(out, y_row[0:1, :]).then_inc(y_stored, 16)
            sp.wait_ge(y_stored, 16)

        @block.gpsimd
        def _(pool):
            pool.wait_ge(ids_loaded, 16)
            with pool.Fori(0, CHUNKS) as c:
                pool.tensor_tensor(rows_now[0:GATHER, :],
                                   all_ids[0:GATHER, bass.ds(c, 1), :].rearrange("p c q -> p (c q)"),
                                   all_ids[0:GATHER, CHUNKS, :], ALU.add).then_inc(rows_made, 1)
                wait_alone(pool, "pool", rows_made, c + 1)
                for q in range(GATHERS):
                    pool.indirect_dma_start(
                        out=gathered[0:GATHER, q, :], out_offset=None, in_=table,
                        in_offset=bass.IndirectOffsetOnAxis(ap=rows_now[0:GATHER, q:q + 1].bitcast(U32), axis=0),
                    ).then_inc(rows_gathered, 16)
                wait_alone(pool, "pool", rows_gathered, c * (16 * GATHERS) + 16 * GATHERS)
                pool.dma_start(x_rows[bass.ds(c, 1), 0:FIELDS, :].rearrange("c f (b d) -> (c f b) d", d=DIM)
                               .rearrange("(q p) d -> p q d", p=GATHER),
                               gathered[0:GATHER]).then_inc(rows_stored, 16)
                whole_gather = GATHER // CHUNK_BATCH
                for q, count in enumerate((whole_gather, REPEATED - whole_gather)):
                    first = FIELDS + whole_gather * q
                    rows = x_rows[bass.ds(c, 1), first:first + count, :]
                    pool.dma_start(rows.rearrange("c f (b d) -> (c f b) d", d=DIM),
                                   gathered[0:count * CHUNK_BATCH, q, :]).then_inc(rows_stored, 16)
                wait_alone(pool, "pool", rows_stored, c * (16 * ROW_STORES) + 16 * ROW_STORES)

        @block.scalar
        def _(act):
            def split_weights(pieces):
                for n in pieces:
                    layer, unit = PIECES[n]
                    if layer == 0:
                        act.wait_ge(w0_folded, n + 1)
                    else:
                        act.wait_ge(raw_loaded[n % RAWS], 16 * (n // RAWS) + 16)
                    rows = slice(0, ROWS_OF_LAYER[layer])
                    act.activation(w[layer][rows, split_places(layer, unit), 0, :],
                                   raw[n % RAWS][rows, 0:tiles_in(layer, unit)], ACT.Copy).then_inc(w_hi_made, 1)

            def make_hi(p, n):
                act.wait_ge(products_made, p.unit(n) + 1)
                if p.before_in_slot(n) is not None:
                    act.wait_ge(units_mixed, p.before_in_slot(n))
                act.activation(z_hi[p.slot(n)][unit_area(p, n)], z[p.slot(n)][unit_area(p, n)], ACT.Copy
                               ).then_inc(hi_made, 1)

            def copy_cross(p):
                act.wait_ge(units_mixed, p.all_units())
                act.activation(cross[:], mix[p.bank][:, :, MIX:2 * MIX], ACT.Copy).then_inc(cross_copied, 1)

            def activate(p):
                act.wait_ge(passes_turned, p.number() + 1)
                if p.layer < 2:
                    if not p.fixed or p.chunk > 0:
                        act.wait_ge(hidden_stored[p.layer], p.chunk * 16)
                    act.activation(hidden_out[p.layer][0:HIDDEN, :], turned(p)[:, 0], ACT.Relu,
                                   bias=bias[0:HIDDEN, p.layer, 0:1]).then_inc(hidden_activated[p.layer], 1)

            def sum_direct(p, half, first):
                row = 2 + half if p.layer == 2 else p.layer
                for b in range(first, first + SUM_BATCH):
                    columns = turned(p)[:, half, DIM * b:DIM * (b + 1)]
                    last = act.activation(columns, columns, ACT.Relu, bias=bias[0:HIDDEN, p.layer, half:half + 1],
                                          accum_out=mixed[0:HIDDEN, row, bass.ds(p.chunk * CHUNK_BATCH + b, 1)])
                if (half, first + SUM_BATCH) == (1, CHUNK_BATCH):
                    last.then_inc(passes_summed, 1)

            def run(segment):
                for p, n, _, _, ended, pieces in segment.timeline():
                    if ACTIVATE in ended:
                        activate(ended[ACTIVATE])
                    if ADD in ended:
                        copy_cross(ended[ADD])
                    if p and not p.whole(n):
                        make_hi(p, n)
                    for distance in sorted(ended, reverse=True):
                        for half, first in sums_at(ended[distance], distance):
                            sum_direct(ended[distance], half, first)
                    split_weights(pieces)

            split_weights(PIECES_BEFORE)
            act.wait_ge(small_loaded, 16 * 5)
            run_segments(act, run)

            act.wait_ge(products_made, CHUNKS * UNITS_PER_STEP)
            act.dma_start(top2[:], w_top2.rearrange("(k p) n -> p k n", p=P)).then_inc(top23_loaded, 16)
            act.dma_start(top3[:], w_top3).then_inc(top23_loaded, 16)
            for m in range(TOP1 // P):
                act.wait_ge(t1_mixed, m + 1)
                act.activation(t1[:, m], t1_bank(m), ACT.Relu, bias=top1_bias[:, m:m + 1]).then_inc(t1_made, 1)
            for m in range(TOP2 // P):
                act.wait_ge(t2_mixed, m + 1)
                act.activation(t2[:, m], mix[2][:, m], ACT.Relu, bias=top2_bias[:, m:m + 1]).then_inc(t2_made, 1)
            act.wait_ge(y_mixed, 1)
            act.activation(y_row[0:1, :], mix[3][0:1, 0, :], ACT.Copy).then_inc(y_made, 1)

        @block.vector
        def _(dve):
            for n in range(UNITS_OF_LAYER[0]):
                dve.wait_ge(raw_loaded[n], 16)
                dve.wait_ge(mirror_loaded, 16 * UNITS_OF_LAYER[0])
                area = slice(0, PAIR_ROWS), slice(0, tiles_in(0, n))
                dve.tensor_tensor(raw[n][area], raw[n][area], mirror[n][area], ALU.add).then_inc(w0_folded, 1)

            def split_weights(pieces):
                for n in pieces:
                    layer, unit = PIECES[n]
                    rows = slice(0, ROWS_OF_LAYER[layer])
                    split = w[layer][rows, split_places(layer, unit)]
                    dve.wait_ge(w_hi_made, n + 1)
                    dve.tensor_tensor(split[:, :, 1, :], raw[n % RAWS][rows, 0:tiles_in(layer, unit)],
                                      split[:, :, 0, :].bitcast(F32), ALU.subtract).then_inc(w_lo_made, 1)

            def make_products(p, n):
                j, i = divmod(n * UNIT, FIELD_TILES)
                if p.layer == 0:
                    if n == 0:
                        dve.wait_ge(pairs_loaded, p.chunk * (16 * PAIR_LOADS) + 16 * PAIR_LOADS)
                    factors, other = partner_tiles(p.chunk, p.like)[n][unit_area(p, n)], single[0:PAIR_ROWS, :]
                else:
                    if n == 0:
                        dve.wait_ge(hidden_loaded[p.layer - 1], p.chunk * 16 + 16)
                        if p.fixed and p.chunk == 0:
                            dve.wait_ge(fields_loaded, 16)
                    if p.fixed and (p.layer, p.chunk, n) == (1, 0, p.units - 1):
                        dve.wait_ge(fields_loaded, 32)
                    if p.layer == 2 and n == p.units - 2 and not (p.fixed and p.chunk > CHUNKS - 3):
                        dve.wait_ge(fields_loaded, p.chunk * 16 + 48)
                    factors = fields[p.like % SLOTS][0:ROWS, i:i + UNIT, :]
                    other = hidden_of(Pass(p.layer - 1, p.chunk, p.like))[0:ROWS, j, :]
                if p.whole(n):
                    if p.before_in_slot(n) is not None:
                        dve.wait_ge(units_mixed, p.before_in_slot(n))
                elif not p.fixed or p.split(n) >= SLOTS:
                    dve.wait_ge(lo_made, p.split(n) + 1 - SLOTS)
                place = z_whole if p.whole(n) else z[p.slot(n)]
                rows, tiles = unit_area(p, n)
                dve.tensor_tensor(place[rows, tiles], factors,
                                  other.unsqueeze(1).to_broadcast([rows.stop, tiles.stop, CHUNK]),
                                  ALU.mult).then_inc(products_made, 1)

            def make_lo(p, n):
                dve.wait_ge(hi_made, p.split(n) + 1)
                if p.before_in_slot(n) is not None:
                    dve.wait_ge(units_mixed, p.before_in_slot(n))
                area = unit_area(p, n)
                dve.tensor_tensor(z_lo[p.slot(n)][area], z[p.slot(n)][area], z_hi[p.slot(n)][area].bitcast(F32),
                                  ALU.subtract).then_inc(lo_made, 1)

            def add_cross(p):
                dve.wait_ge(cross_copied, p.number() + 1)
                if not p.fixed or p.number() > 0:
                    dve.wait_ge(passes_turned, p.number())
                dve.tensor_tensor(total[:], mix[p.bank][:, :, 0:MIX], cross[:], ALU.add).then_inc(totals_made, 1)

            def run(segment):
                if segment.fresh:
                    make_products(segment.runs[0].p, 0)
                for p, n, q, m, ended, pieces in segment.timeline():
                    if q:
                        make_products(q, m)
                    if ADD in ended:
                        add_cross(ended[ADD])
                    if p and not p.whole(n):
                        make_lo(p, n)
                    split_weights(pieces)

            split_weights(PIECES_BEFORE)
            run_segments(dve, run)

        @block.tensor
        def _(pe):
            def mix_unit(p, n):
                if n == 0 and p.before_in_banks() is not None:
                    pe.wait_ge(passes_summed, p.before_in_banks())
                if p.fixed and p.chunk == 0 and not p.whole(n):
                    pe.wait_ge(w_lo_made, PIECES.index((p.layer, n)) + 1)
                if p.whole(n):
                    pe.wait_ge(products_made, p.unit(n) + 1)
                    if p.fixed:
                        pe.wait_ge(whole_loaded, 16 * len(WHOLE))
                    for k in range(UNIT):
                        for b in range(BLOCKS):
                            mm = pe.matmul(mix[p.bank][:, b, 0:MIX], z_whole[0:ROWS, k, P * b:P * (b + 1)],
                                           w_whole[0:ROWS, list(WHOLE).index(p.layer), k, :], start=False,
                                           stop=(n == p.units - 1 and k == UNIT - 1), skip_group_check=True)
                    mm.then_inc(units_mixed, 1)
                    return
                rows = slice(0, ROWS_OF_LAYER[p.layer])
                weights = w[p.layer][rows, split_places(p.layer, n)]
                last_tile = tiles_in(p.layer, n) - 1
                for made, part, columns in ((hi_made, z_hi, 2), (lo_made, z_lo, 1)):
                    pe.wait_ge(made, p.split(n) + 1)
                    for k in range(last_tile + 1):
                        for b in range(BLOCKS):
                            mm = pe.matmul(mix[p.bank][:, b, 0:columns * MIX],
                                           part[p.slot(n)][rows, k, P * b:P * (b + 1)],
                                           weights[:, k, 0:columns, :].rearrange("p c n -> p (c n)"),
                                           start=(n == 0 and k == 0 and part is z_hi),
                                           stop=(n == p.units - 1 and k == last_tile and part is z_lo),
                                           skip_group_check=True)
                mm.then_inc(units_mixed, 1)

            def turn(p):
                pe.wait_ge(totals_made, p.number() + 1)
                for b in range(BLOCKS):
                    for half in range(2):
                        last = pe.transpose(turned(p)[:, half, P * b:P * (b + 1)],
                                            total[:, b, HIDDEN * half:HIDDEN * (half + 1)], ident[:])
                last.then_inc(passes_turned, 1)

            def run(segment):
                for p, n, _, _, ended, pieces in segment.timeline():
                    if TURN in ended:
                        turn(ended[TURN])
                    if p:
                        mix_unit(p, n)

            pe.wait_ge(small_loaded, 16 * 5)
            run_segments(pe, run)

            pe.wait_ge(top1_loaded, 16)
            pe.wait_ge(passes_summed, NUMBER[1, CHUNKS - 1] + 1)
            for m in range(TOP1 // P):
                for k in range(2):
                    pe.matmul(t1_bank(m), top1[0:TOP1_ROWS, k, P * m:P * (m + 1)], mixed[0:TOP1_ROWS, k, :],
                              start=(k == 0), stop=False)
            pe.wait_ge(passes_summed, len(ORDER))
            for m in range(TOP1 // P):
                for k in range(2, 4):
                    mm = pe.matmul(t1_bank(m), top1[0:TOP1_ROWS, k, P * m:P * (m + 1)], mixed[0:TOP1_ROWS, k, :],
                                   start=False, stop=(k == 3))
                mm.then_inc(t1_mixed, 1)
            pe.wait_ge(top23_loaded, 16 * 2)
            for m in range(TOP2 // P):
                for k in range(TOP1 // P):
                    if m == 0:
                        pe.wait_ge(t1_made, k + 1)
                    mm = pe.matmul(mix[2][:, m], top2[:, k, P * m:P * (m + 1)], t1[:, k], start=(k == 0),
                                   stop=(k == TOP1 // P - 1))
                mm.then_inc(t2_mixed, 1)
            for k in range(TOP2 // P):
                pe.wait_ge(t2_made, k + 1)
                mm = pe.matmul(mix[3][0:1, 0, :], top3[:, k:k + 1], t2[:, k], start=(k == 0), stop=(k == TOP2 // P - 1))
            mm.then_inc(y_mixed, 1)


def lay_out(inputs):
    import numpy as np

    def given(name):
        return np.asarray(inputs[name])

    tables = [given(f"tbl_{f}") for f in range(FIELDS)]
    starts = np.cumsum([0] + [t.shape[0] for t in tables[:-1]]).astype(np.int32)
    by_row = np.repeat(starts, CHUNK_BATCH).reshape(GATHERS, GATHER)
    by_chunk = given("ids").reshape(CHUNKS, CHUNK_BATCH, FIELDS).transpose(0, 2, 1).reshape(CHUNKS, GATHERS, GATHER)
    arrays = {
        "table": np.concatenate(tables),
        "context_t": np.ascontiguousarray(given("dense_ctx").T.reshape(4, -1, BATCH).transpose(1, 0, 2)),
        "ids": np.ascontiguousarray(np.concatenate([by_chunk, by_row[None]]).transpose(2, 0, 1)),
        "identity": np.eye(P, dtype=np.float32),
    }
    raw = given("L0_rec_W0").reshape(FIELDS, FIELDS, MIX)
    w0 = np.zeros((TURNS, FIELDS, PARTNER_TILES, MIX), raw.dtype)
    w0_mirror = np.zeros_like(w0)
    m = np.arange(FIELDS)
    for distance in range(DISTANCES):
        turn, tile = divmod(distance, PARTNER_TILES)
        partner = (m + distance) % FIELDS
        w0[turn, :, tile] = raw[m, partner]
        if distance:
            w0_mirror[turn, :, tile] = raw[partner, m]
    arrays["w0"], arrays["w0_mirror"] = (a.reshape(PAIR_ROWS, PARTNER_TILES, MIX) for a in (w0, w0_mirror))
    for layer in (1, 2):
        raw = given(f"L0_rec_W{layer}").reshape(FIELDS, HIDDEN, MIX)
        padded = np.zeros((GROUPS * FIELD_TILES, HIDDEN, MIX), raw.dtype)
        padded[:FIELDS] = raw
        tiled = padded.reshape(GROUPS, FIELD_TILES, LANES, HIDDEN_TILES, MIX).transpose(0, 2, 3, 1, 4)
        arrays[f"w{layer}"] = np.ascontiguousarray(tiled.reshape(ROWS, -1, MIX))
    biases = np.stack([given(f"L0_rec_b{n}") for n in range(3)])
    arrays["biases"] = np.ascontiguousarray(biases.reshape(3, 2, HIDDEN).transpose(2, 0, 1))
    raw = given("W_top1")
    of_mixed, of_context = (a.reshape(4, -1, TOP1) for a in (raw[:4 * HIDDEN], raw[4 * HIDDEN:]))
    arrays["w_top1"] = np.ascontiguousarray(np.concatenate([of_mixed, of_context], axis=1).transpose(1, 0, 2))
    arrays["b_top1"] = np.ascontiguousarray(given("b_top1").reshape(TOP1 // P, P).T)
    arrays["w_top2"] = given("W_top2")
    arrays["b_top2"] = np.ascontiguousarray(given("b_top2").reshape(TOP2 // P, P).T)
    arrays["w_top3"] = np.ascontiguousarray(given("W_top3").reshape(TOP2 // P, P).T)
    return arrays


def kernel(**inputs):
    import concourse.bacc as bacc
    from concourse.bass_utils import run_bass_kernel_spmd

    nc = bacc.Bacc("TRN2", target_bir_lowering=False, num_devices=1)
    arrays = lay_out(inputs)
    aps = {name: nc.dram_tensor(name, a.shape, mybir.dt.from_np(a.dtype), kind="ExternalInput").ap()
           for name, a in arrays.items()}
    out = nc.dram_tensor("out", (BATCH, 1), F32, kind="ExternalOutput").ap()
    tower(nc, out=out.rearrange("b one -> one b"), **aps)
    result = run_bass_kernel_spmd(nc, [arrays], core_ids=[0])
    return result.results[0]["out"]
```
